# Optimizing a Trainium2 kernel written in Bass

```python
import numpy as np
import jax
import jax.numpy as jnp

def _softmax(x, axis=-1):
    return jax.nn.softmax(x, axis=axis)

def _gelu(x):
    return jax.nn.gelu(x, approximate=True)

def _silu(x):
    return jax.nn.silu(x)

def _sigmoid(x):
    return jax.nn.sigmoid(x)

def _layernorm(x, axis=-1, eps=1e-05):
    m = jnp.mean(x, axis=axis, keepdims=True)
    v = jnp.var(x, axis=axis, keepdims=True)
    return (x - m) / jnp.sqrt(v + eps)

def _scatter_add(tgt, idx, src, axis=0):
    return tgt.at[idx].add(src)

def _segment_sum(src, seg, n):
    return jax.ops.segment_sum(src, seg, n)
kernel_name = 'mk_xattn_ffn_d1_seqx_r4_aa7a8a'

def setup_inputs(seed: int=0):
    np.random.seed(seed)
    _w = jnp.asarray

    def _rec_inputs():
        import jax
        import jax.numpy as jnp
        _rk = jax.random.key(seed)
        x = -4.161e-06 + 1 * jax.random.normal(jax.random.fold_in(_rk, 1), (4, 512, 512), jnp.float32)
        _lenS = 512 - jax.random.randint(jax.random.fold_in(_rk, 7), (4,), 0, max(1, 512 // 4) + 1, jnp.int32)
        _lenS2 = 512 - jax.random.randint(jax.random.fold_in(_rk, 8), (4,), 0, max(1, 512 // 4) + 1, jnp.int32)
        _ctx_2048P = jax.random.normal(jax.random.fold_in(_rk, 11), (4, 16, 512), jnp.float32)
        _ctx_2048c = jax.random.dirichlet(jax.random.fold_in(_rk, 511), 0.3 * jnp.ones((16,), jnp.float32), (4, 512))
        _ctx_2048t = jnp.einsum('bsk,bkd->bsd', _ctx_2048c, _ctx_2048P)
        _ctx_2048t = _ctx_2048t * jax.lax.rsqrt(jnp.mean(jnp.square(_ctx_2048t)) + 1e-12) * 0.953939
        ctx_2048 = -0.000192764 + 0.999654 * (_ctx_2048t + 0.3 * jax.random.normal(jax.random.fold_in(_rk, 611), (4, 512, 512), jnp.float32))
        return (x, ctx_2048)
    x, ctx_2048 = _rec_inputs()

    def _L0_xattn_setup():
        import jax, jax.numpy as jnp
        import numpy as np
        FP8_MAX = 448.0
        EPS = 1e-05

        def _fp8_roundtrip(x):
            return x.astype(jnp.float8_e4m3fn).astype(jnp.float32)

        def _div_clamp_fp8(x, scale):
            y = jnp.clip(x.astype(jnp.float32) / scale, -FP8_MAX, FP8_MAX)
            y = y.astype(jnp.bfloat16).astype(jnp.float32)
            return _fp8_roundtrip(y)

        def _ln(x, w, b):
            mu = jnp.mean(x, axis=-1, keepdims=True)
            var = jnp.mean(jnp.square(x - mu), axis=-1, keepdims=True)
            return (x - mu) * jax.lax.rsqrt(var + EPS) * w + b

        def _fp8_linear_pertensor(x, wq, w_scale, in_scale):
            xq = _div_clamp_fp8(x, in_scale)
            return jnp.einsum('bsi,oi->bso', xq * in_scale, wq) * w_scale

        def _gqa(q, k, v):
            scale = 1.0 / np.sqrt(q.shape[-1])
            scores = jnp.einsum('bsghd,btgd->bghst', q, k) * scale
            p = jax.nn.softmax(scores, axis=-1)
            return jnp.einsum('bghst,btgd->bsghd', p, v)
        key = jax.random.key(seed)
        ks = jax.random.split(key, 8)
        B, S, SC, H, NH, G, D = (2, 512, 128, 512, 16, 8, 128)

        def qw(k, out_f, in_f):
            w = jax.random.normal(k, (out_f, in_f), jnp.float32) * 0.02
            sc = jnp.max(jnp.abs(w)) / FP8_MAX
            return (_fp8_roundtrip(w / sc), sc.astype(jnp.float32))
        wq, wq_s = qw(ks[0], NH * D, H)
        wqx, wqx_s = qw(ks[1], NH * D, H)
        wk, wk_s = qw(ks[2], G * D, H)
        wv, wv_s = qw(ks[3], G * D, H)
        wproj, wp_s = qw(ks[4], H, 2 * NH * D)
        return {'hidden_states': jax.random.normal(ks[5], (B, S, H), jnp.float32), 'cond': jax.random.normal(ks[6], (B, SC, H), jnp.float32), 'ln_w': jnp.ones((H,), jnp.float32), 'ln_b': jnp.zeros((H,), jnp.float32), 'wq': wq, 'wq_scale': wq_s, 'q_in_scale': jnp.full((H,), 0.05, jnp.float32), 'wqx': wqx, 'wqx_scale': wqx_s, 'qx_in_scale': jnp.full((H,), 0.05, jnp.float32), 'wk': wk, 'wk_scale': wk_s, 'k_in_scale': jnp.full((H,), 0.05, jnp.float32), 'wv': wv, 'wv_scale': wv_s, 'v_in_scale': jnp.full((H,), 0.05, jnp.float32), 'w_kv_x': jax.random.normal(ks[7], (2 * G * D, H), jnp.float32) * 0.02, 'qln_w': jnp.ones((D,), jnp.float32), 'qln_b': jnp.zeros((D,), jnp.float32), 'kln_w': jnp.ones((D,), jnp.float32), 'kln_b': jnp.zeros((D,), jnp.float32), 'qxln_w': jnp.ones((D,), jnp.float32), 'qxln_b': jnp.zeros((D,), jnp.float32), 'kxln_w': jnp.ones((D,), jnp.float32), 'kxln_b': jnp.zeros((D,), jnp.float32), 'wproj': wproj, 'proj_w_scale': wp_s, 'proj_in_scale': jnp.asarray(0.05, jnp.float32), 'proj_smooth': jnp.full((2 * NH * D,), 0.05, jnp.float32)}
    _L0_xattn_all = _L0_xattn_setup()
    _L0_xattn_in = {k: v for k, v in _L0_xattn_all.items() if k in ('ln_w', 'ln_b', 'wq', 'wq_scale', 'q_in_scale', 'wqx', 'wqx_scale', 'qx_in_scale', 'wk', 'wk_scale', 'k_in_scale', 'wv', 'wv_scale', 'v_in_scale', 'w_kv_x', 'qln_w', 'qln_b', 'kln_w', 'kln_b', 'qxln_w', 'qxln_b', 'kxln_w', 'kxln_b', 'wproj', 'proj_w_scale', 'proj_in_scale', 'proj_smooth')}
    del _L0_xattn_all

    def _L0_ffn_setup():
        import jax, jax.numpy as jnp
        import numpy as np
        DIM = 512
        HID = 1408
        ZERO_POINT = 128.0

        def _qlinear(x, wq, scale):
            W = (wq.astype(jnp.float32) - ZERO_POINT) * scale[:, None]
            return jnp.einsum('bsd,hd->bsh', x, W)
        key = jax.random.key(seed)
        ks = jax.random.split(key, 7)
        B, S = (4, 512)
        sg = jax.random.uniform(ks[1], (HID,)) * (0.02 / np.sqrt(DIM)) + 0.0001
        su = jax.random.uniform(ks[3], (HID,)) * (0.02 / np.sqrt(DIM)) + 0.0001
        sd = jax.random.uniform(ks[5], (DIM,)) * (0.02 / np.sqrt(HID)) + 0.0001
        return {'x': jax.random.normal(ks[0], (B, S, DIM), dtype=jnp.float32), 'wq_gate': jax.random.randint(ks[2], (HID, DIM), 0, 64, dtype=jnp.int32), 's_gate': sg, 'wq_up': jax.random.randint(ks[4], (HID, DIM), 0, 64, dtype=jnp.int32), 's_up': su, 'wq_down': jax.random.randint(ks[6], (DIM, HID), 0, 64, dtype=jnp.int32), 's_down': sd}
    _L0_ffn_all = _L0_ffn_setup()
    _L0_ffn_in = {k: v for k, v in _L0_ffn_all.items() if k in ('wq_gate', 's_gate', 'wq_up', 's_up', 'wq_down', 's_down')}
    del _L0_ffn_all
    return {'x': x, 'ctx_2048': ctx_2048, 'L0_xattn_ln_w': _L0_xattn_in['ln_w'], 'L0_xattn_ln_b': _L0_xattn_in['ln_b'], 'L0_xattn_wq': _L0_xattn_in['wq'], 'L0_xattn_wq_scale': _L0_xattn_in['wq_scale'], 'L0_xattn_q_in_scale': _L0_xattn_in['q_in_scale'], 'L0_xattn_wqx': _L0_xattn_in['wqx'], 'L0_xattn_wqx_scale': _L0_xattn_in['wqx_scale'], 'L0_xattn_qx_in_scale': _L0_xattn_in['qx_in_scale'], 'L0_xattn_wk': _L0_xattn_in['wk'], 'L0_xattn_wk_scale': _L0_xattn_in['wk_scale'], 'L0_xattn_k_in_scale': _L0_xattn_in['k_in_scale'], 'L0_xattn_wv': _L0_xattn_in['wv'], 'L0_xattn_wv_scale': _L0_xattn_in['wv_scale'], 'L0_xattn_v_in_scale': _L0_xattn_in['v_in_scale'], 'L0_xattn_w_kv_x': _L0_xattn_in['w_kv_x'], 'L0_xattn_qln_w': _L0_xattn_in['qln_w'], 'L0_xattn_qln_b': _L0_xattn_in['qln_b'], 'L0_xattn_kln_w': _L0_xattn_in['kln_w'], 'L0_xattn_kln_b': _L0_xattn_in['kln_b'], 'L0_xattn_qxln_w': _L0_xattn_in['qxln_w'], 'L0_xattn_qxln_b': _L0_xattn_in['qxln_b'], 'L0_xattn_kxln_w': _L0_xattn_in['kxln_w'], 'L0_xattn_kxln_b': _L0_xattn_in['kxln_b'], 'L0_xattn_wproj': _L0_xattn_in['wproj'], 'L0_xattn_proj_w_scale': _L0_xattn_in['proj_w_scale'], 'L0_xattn_proj_in_scale': _L0_xattn_in['proj_in_scale'], 'L0_xattn_proj_smooth': _L0_xattn_in['proj_smooth'], 'L0_ffn_wq_gate': _L0_ffn_in['wq_gate'], 'L0_ffn_s_gate': _L0_ffn_in['s_gate'], 'L0_ffn_wq_up': _L0_ffn_in['wq_up'], 'L0_ffn_s_up': _L0_ffn_in['s_up'], 'L0_ffn_wq_down': _L0_ffn_in['wq_down'], 'L0_ffn_s_down': _L0_ffn_in['s_down']}

def reference(x, ctx_2048, L0_xattn_ln_w, L0_xattn_ln_b, L0_xattn_wq, L0_xattn_wq_scale, L0_xattn_q_in_scale, L0_xattn_wqx, L0_xattn_wqx_scale, L0_xattn_qx_in_scale, L0_xattn_wk, L0_xattn_wk_scale, L0_xattn_k_in_scale, L0_xattn_wv, L0_xattn_wv_scale, L0_xattn_v_in_scale, L0_xattn_w_kv_x, L0_xattn_qln_w, L0_xattn_qln_b, L0_xattn_kln_w, L0_xattn_kln_b, L0_xattn_qxln_w, L0_xattn_qxln_b, L0_xattn_kxln_w, L0_xattn_kxln_b, L0_xattn_wproj, L0_xattn_proj_w_scale, L0_xattn_proj_in_scale, L0_xattn_proj_smooth, L0_ffn_wq_gate, L0_ffn_s_gate, L0_ffn_wq_up, L0_ffn_s_up, L0_ffn_wq_down, L0_ffn_s_down):
    import jax
    import jax.numpy as jnp

    def _L0_xattn_ref(hidden_states, cond, ln_w, ln_b, wq, wq_scale, q_in_scale, wqx, wqx_scale, qx_in_scale, wk, wk_scale, k_in_scale, wv, wv_scale, v_in_scale, w_kv_x, qln_w, qln_b, kln_w, kln_b, qxln_w, qxln_b, kxln_w, kxln_b, wproj, proj_w_scale, proj_in_scale, proj_smooth):
        import jax, jax.numpy as jnp
        import numpy as np
        FP8_MAX = 448.0
        EPS = 1e-05

        def _fp8_roundtrip(x):
            return x.astype(jnp.float8_e4m3fn).astype(jnp.float32)

        def _div_clamp_fp8(x, scale):
            y = jnp.clip(x.astype(jnp.float32) / scale, -FP8_MAX, FP8_MAX)
            y = y.astype(jnp.bfloat16).astype(jnp.float32)
            return _fp8_roundtrip(y)

        def _ln(x, w, b):
            mu = jnp.mean(x, axis=-1, keepdims=True)
            var = jnp.mean(jnp.square(x - mu), axis=-1, keepdims=True)
            return (x - mu) * jax.lax.rsqrt(var + EPS) * w + b

        def _fp8_linear_pertensor(x, wq, w_scale, in_scale):
            xq = _div_clamp_fp8(x, in_scale)
            return jnp.einsum('bsi,oi->bso', xq * in_scale, wq) * w_scale

        def _gqa(q, k, v):
            scale = 1.0 / np.sqrt(q.shape[-1])
            scores = jnp.einsum('bsghd,btgd->bghst', q, k) * scale
            p = jax.nn.softmax(scores, axis=-1)
            return jnp.einsum('bghst,btgd->bsghd', p, v)
        b, s, _ = hidden_states.shape
        sc = cond.shape[1]
        d = qln_w.shape[0]
        nh = wq.shape[0] // d
        g = wk.shape[0] // d
        hpg = nh // g
        ln_out = _ln(hidden_states, ln_w, ln_b)
        q = _fp8_linear_pertensor(ln_out, wq, wq_scale, q_in_scale).reshape(b, s, g, hpg, d)
        q = _ln(q, qln_w, qln_b)
        k = _fp8_linear_pertensor(ln_out, wk, wk_scale, k_in_scale).reshape(b, s, g, d)
        k = _ln(k, kln_w, kln_b)
        v = _fp8_linear_pertensor(ln_out, wv, wv_scale, v_in_scale).reshape(b, s, g, d)
        core = _gqa(q, k, v).reshape(b, s, nh * d)
        qx = _fp8_linear_pertensor(ln_out, wqx, wqx_scale, qx_in_scale).reshape(b, s, g, hpg, d)
        qx = _ln(qx, qxln_w, qxln_b)
        kvx = jnp.einsum('bsi,oi->bso', cond, w_kv_x)
        kx, vx = jnp.split(kvx, 2, axis=-1)
        kx = _ln(kx.reshape(b, sc, g, d), kxln_w, kxln_b)
        vx = vx.reshape(b, sc, g, d)
        xout = _gqa(qx, kx, vx).reshape(b, s, nh * d)
        cat = jnp.concatenate([core, xout], axis=-1)
        catq = _div_clamp_fp8(cat, proj_smooth)
        return jnp.einsum('bsi,oi->bso', catq, wproj) * (proj_in_scale * proj_w_scale)

    def _L0_ffn_ref(x, wq_gate, s_gate, wq_up, s_up, wq_down, s_down):
        import jax, jax.numpy as jnp
        import numpy as np
        DIM = 512
        HID = 1408
        ZERO_POINT = 128.0

        def _qlinear(x, wq, scale):
            W = (wq.astype(jnp.float32) - ZERO_POINT) * scale[:, None]
            return jnp.einsum('bsd,hd->bsh', x, W)
        gate = _qlinear(x, wq_gate, s_gate)
        gate = jax.nn.silu(gate)
        up = _qlinear(x, wq_up, s_up)
        return _qlinear(gate * up, wq_down, s_down)
    x = x + _L0_xattn_ref(_layernorm(x, axis=-1), ctx_2048, L0_xattn_ln_w, L0_xattn_ln_b, L0_xattn_wq, L0_xattn_wq_scale, L0_xattn_q_in_scale, L0_xattn_wqx, L0_xattn_wqx_scale, L0_xattn_qx_in_scale, L0_xattn_wk, L0_xattn_wk_scale, L0_xattn_k_in_scale, L0_xattn_wv, L0_xattn_wv_scale, L0_xattn_v_in_scale, L0_xattn_w_kv_x, L0_xattn_qln_w, L0_xattn_qln_b, L0_xattn_kln_w, L0_xattn_kln_b, L0_xattn_qxln_w, L0_xattn_qxln_b, L0_xattn_kxln_w, L0_xattn_kxln_b, L0_xattn_wproj, L0_xattn_proj_w_scale, L0_xattn_proj_in_scale, L0_xattn_proj_smooth)
    x = x + _L0_ffn_ref(_layernorm(x, axis=-1), L0_ffn_wq_gate, L0_ffn_s_gate, L0_ffn_wq_up, L0_ffn_s_up, L0_ffn_wq_down, L0_ffn_s_down)
    return x

_drawn_inputs = setup_inputs


def setup_inputs(seed=0):
    import zlib

    import numpy as np

    out = dict(_drawn_inputs(seed))
    spreads = {'L0_xattn_ln_w': (1.0, 0.6),
     'L0_xattn_ln_b': (0.0, 0.1),
     'L0_xattn_q_in_scale': (0.05000000074505806, 0.6),
     'L0_xattn_qx_in_scale': (0.05000000074505806, 0.6),
     'L0_xattn_k_in_scale': (0.05000000074505806, 0.6),
     'L0_xattn_v_in_scale': (0.05000000074505806, 0.6),
     'L0_xattn_qln_w': (1.0, 0.6),
     'L0_xattn_qln_b': (0.0, 0.8),
     'L0_xattn_kln_w': (1.0, 0.6),
     'L0_xattn_kln_b': (0.0, 0.8),
     'L0_xattn_qxln_w': (1.0, 0.6),
     'L0_xattn_qxln_b': (0.0, 0.692),
     'L0_xattn_kxln_w': (1.0, 0.6),
     'L0_xattn_kxln_b': (0.0, 0.8),
     'L0_xattn_proj_smooth': (0.05000000074505806, 0.2)}
    factors = {'L0_ffn_s_up': 2.936, 'L0_ffn_s_down': 3.076}
    for name, (base, spread) in spreads.items():
        noise = np.random.default_rng([zlib.crc32(name.encode()), seed]).standard_normal(out[name].shape)
        drawn = base * np.exp(spread * noise) if base else spread * noise
        out[name] = jnp.asarray(drawn.astype(out[name].dtype))
    for name, factor in factors.items():
        out[name] = (out[name] * factor).astype(out[name].dtype)
    return out
```

```python
from contextlib import ExitStack

import numpy as np

import concourse.bass as bass
from concourse import mybir

F32 = mybir.dt.float32
BF16 = mybir.dt.bfloat16
I16 = mybir.dt.int16
I32 = mybir.dt.int32
ALU = mybir.AluOpType
ACT = mybir.ActivationFunctionType
AX_X = mybir.AxisListType.X

P = 128
B, T, DM = 4, 512, 512
NTOK = B * T
G, D = 8, 128
HPG = 2
NH = G * HPG
CH = DM // P
TT = T // P
HID = 1408
HC = HID // P
SETS = 4
GW = 8 * D
HEADS = 2 * HPG
UNITS = HEADS * TT
TILES = 2 * TT
EPS = 1e-5
FP8_MAX = 448.0
EXPONENT = 0x7F80
MIN_BINADE = 2.0 ** -6
KEEP4 = 24.0

FREE = 1

COLS = {}
for _name, _n in (("ln_w", CH), ("ln_b", CH), ("in_scale", SETS * CH), ("w_scale", SETS), ("qln_w", 1), ("qln_b", 1),
                  ("qxln_w", 1), ("qxln_b", 1), ("kln_w", 1), ("kln_b", 1), ("kxln_w", 1), ("kxln_b", 1),
                  ("smooth", NH * 2), ("s_gate", HC), ("s_up", HC), ("proj_in", 1), ("proj_w", 1)):
    COLS[_name] = (sum(n for _, n in COLS.values()), _n)
NCOLS = sum(n for _, n in COLS.values())


def block_kernel(nc, x, ctx_t, w_group, w_proj, w_gate, w_up, w_down, cols, s_down, out):
    x_tiles = x.rearrange("(b t p) d -> b p t d", b=B, p=P)
    out_tiles = out.rearrange("(b t p) d -> b t p d", b=B, p=P)
    ctx_chunks = ctx_t.rearrange("(c p) t -> c p t", p=P)
    wg_chunks = w_group.rearrange("g (c p) n -> g c p n", p=P)
    heads_dram = nc.dram_tensor("quantised_heads", (B, G, P, HEADS * T), BF16, kind="Internal").ap()

    stack = ExitStack()
    with stack:
        def sb(name, shape, dt):
            return stack.enter_context(nc.sbuf_tensor(name, shape, dt))

        def psum(name):
            return stack.enter_context(nc.psum_tensor(name, [P, 512], F32))

        def sem(name):
            return stack.enter_context(nc.semaphore(name))

        wide = sb("wide", [P, 65536], BF16)
        local = sb("local", [P, 35840], BF16)
        w_raw = sb("w_raw", [P, GW], F32)
        ident = sb("ident", [P, P], F32)
        col = sb("col", [P, NCOLS], F32)
        rscale = sb("rscale", [P, SETS * CH], F32)
        wscale = sb("wscale", [P, CH * 8], F32)
        rsmooth = sb("rsmooth", [P, NH * 2], F32)
        qscaled = sb("qscaled", [P, 4], F32)
        pscale = sb("pscale", [P, 1], F32)
        centre = sb("centre", [P, 8], F32)
        minus_half = sb("minus_half", [P, 8], F32)
        stats = sb("stats", [P, TT, 6], F32)
        moments = sb("moments", [P, TT, 2], F32)
        spread = sb("spread", [P, TT], F32)
        rstd = sb("rstd", [P, TT], F32)
        w_sum = sb("w_sum", [P, 8], F32)
        w_mean = sb("w_mean", [P, 8], F32)
        neg_max = sb("neg_max", [P, 4], F32)
        p_sum = sb("p_sum", [P, 4], F32)
        r_sum = sb("r_sum", [P, 4], F32)
        sq_sum = sb("sq_sum", [P, 2, 4], F32)
        head_var = sb("head_var", [P, 2, 4], F32)
        head_rstd = sb("head_rstd", [P, 2, 4], F32)

        class Carve:
            def __init__(self, region):
                self.region, self.at = region, 0

            def __call__(self, shape, dt):
                n = int(np.prod(shape)) * (2 if dt in (F32, I32) else 1)
                v = self.region[:, self.at:self.at + n]
                self.at += n
                if dt != BF16:
                    v = v.bitcast(dt)
                if len(shape) == 1:
                    return v
                names = "abcde"[:len(shape)]
                return v.rearrange(f"p ({' '.join(names)}) -> p {' '.join(names)}",
                                   **{k: s for k, s in zip(names[1:], shape[1:])})

        def c_(name, i=0, n=1):
            at = COLS[name][0] + i
            return col[:, at:at + n]

        carve = Carve(wide)
        xq = carve([SETS, CH, NTOK], BF16)
        ctx_hi = carve([CH, NTOK], BF16)
        ctx_lo = carve([CH, NTOK], BF16)
        PART, PAR = CH * GW, 2 * CH * GW
        w_bf = carve([2 * PAR], BF16)
        carve = Carve(wide)
        wp = carve([G * HEADS, DM], BF16)
        wgu = carve([CH, 2 * HID], BF16)
        wd = carve([HC, DM], BF16)
        stage = carve([2, 4096], F32)
        h_hi = carve([HC, T], BF16)
        h_lo = carve([HC, T], BF16)
        zt_hi = carve([CH, T], BF16)
        zt_lo = carve([CH, T], BF16)
        carve = Carve(stage.rearrange("p a b -> p (a b)").bitcast(BF16))
        silu = carve([2, T], F32)
        hid = carve([2, T], F32)
        scaled = carve([2, DM], F32)
        carve = Carve(local)
        x_in = carve([2, TT, DM], F32)
        z1 = carve([TT, DM], F32)
        z2 = carve([TT, DM], F32)
        ln_t = carve([2, T], F32)
        y4 = carve([2, SETS * T], BF16)
        mag4 = carve([SETS * T], BF16)
        sum4 = carve([SETS * T], BF16)
        ctx_raw = carve([NTOK], F32)
        carve = Carve(local)
        qk_hi = carve([2, 2, 3, T], BF16)
        qk_lo = carve([2, 2, 3, T], BF16)
        v_hi = carve([2, 2, TT, D], BF16)
        v_lo = carve([2, 2, TT, D], BF16)
        pt_hi = carve([2, TT, T], BF16)
        pt_lo = carve([2, TT, T], BF16)
        heads = carve([HEADS, T], BF16)
        y = carve([2, T], BF16)
        mag = carve([T], BF16)
        summed = carve([T], BF16)
        sq = carve([3 * D], F32)
        qn = carve([2, 3 * D], F32)
        qk_full = carve([3 * D], F32)
        p_exp = carve([2, T], F32)
        p_norm = carve([2, T], F32)
        carve = Carve(local)
        heads_in = carve([G, HEADS, T], BF16)
        x1 = carve([2 * TT * DM], F32)
        x_res = carve([TT, DM], F32)
        z3 = carve([TT, DM], F32)
        y_out = carve([2, DM], F32)
        sdown = carve([DM], F32)

        ps_s = [psum(f"ps_s{i}") for i in range(2)]
        ps_pt = [psum(f"ps_pt{i}") for i in range(2)]
        ps_pj = [psum(f"ps_pj{i}") for i in range(2)]
        ps_qt = psum("ps_qt")
        ps_o = psum("ps_o")
        ps_up = [ps_qt, ps_o]

        waited_act = sem("waited_act")
        waited_dve = sem("waited_dve")
        cols_in = sem("cols_in")
        ident_zero = sem("ident_zero")
        ones_set = sem("ones_set")
        const_ready = sem("const_ready")
        scales_ready = sem("scales_ready")
        x_loaded = sem("x_loaded")
        ctx_loaded = sem("ctx_loaded")
        ctx_hi_done = sem("ctx_hi_done")
        ctx_lo_done = sem("ctx_lo_done")
        ln_step = sem("ln_step")
        ln_var = sem("ln_var")
        ln_rstd = sem("ln_rstd")
        ln_z = sem("ln_z")
        zt_done = sem("zt_done")
        lnt_done = sem("lnt_done")
        y4_done = sem("y4_done")
        quant_step = sem("quant_step")
        xq_done = sem("xq_done")
        w_loaded = sem("w_loaded")
        w_step = sem("w_step")
        w_centred = sem("w_centred")
        w_scaled = sem("w_scaled")
        w_hi_done = sem("w_hi_done")
        w_ready = sem("w_ready")
        proj_done = sem("proj_done")
        sq_done = sem("sq_done")
        vhi_done = sem("vhi_done")
        vlo_done = sem("vlo_done")
        red_done = sem("red_done")
        var_done = sem("var_done")
        rstd_done = sem("rstd_done")
        qn_done = sem("qn_done")
        qt_done = sem("qt_done")
        full_done = sem("full_done")
        qklo_done = sem("qklo_done")
        s_done = sem("s_done")
        max_done = sem("max_done")
        exp_done = sem("exp_done")
        rsum_done = sem("rsum_done")
        norm_done = sem("norm_done")
        pt_done = sem("pt_done")
        pthi_done = sem("pthi_done")
        ptlo_done = sem("ptlo_done")
        pv_done = sem("pv_done")
        y_done = sem("y_done")
        heads_done = sem("heads_done")
        heads_stored = sem("heads_stored")
        stage_loaded = [sem(f"stage_loaded{i}") for i in range(2)]
        stage_done = sem("stage_done")
        sdown_in = sem("sdown_in")
        heads_back = sem("heads_back")
        x_back = sem("x_back")
        pj_done = sem("pj_done")
        x1_done = sem("x1_done")
        z3t_done = sem("z3t_done")
        zthi_done = sem("zthi_done")
        ztlo_done = sem("ztlo_done")
        gate_done = sem("gate_done")
        up_done = sem("up_done")
        silu_done = sem("silu_done")
        hid_done = sem("hid_done")
        hhi_done = sem("hhi_done")
        hlo_done = sem("hlo_done")
        down_done = sem("down_done")
        scaled_done = sem("scaled_done")
        out_ready = sem("out_ready")
        out_stored = [sem(f"out_stored{i}") for i in range(2)]

        LN_STEPS = 2 * TT
        QUANT_STEPS = 4
        N_STAGE, PROJ_PIECES, GATE_UP_PIECES = 10, 4, 4

        SLOTS = B * UNITS
        GROUP_TILES = B * TILES
        GROUP_HEADS = B * HEADS
        EXP_LAG, TURN_LAG, SPLIT_LAG = 1, 3, 4
        PV_LAG, Y_LAG, QUANT_LAG, STORE_LAG = 5, 6, 7, 8
        SQ_LAG, VAR_LAG, QN_LAG, QT_LAG, QK_LAG, REST_LAG = 1, 2, 3, 4, 5, 6
        PREP_FIRST, PREP_STEP = 4, 10
        CENTRE_LAG, SCALE_LAG, HI_LAG, LO_LAG = 1, 3, 5, 6
        TAIL = 4 + STORE_LAG
        STAGE_SLOTS = [SLOTS - UNITS + 2 + 3 * n for n in range(PROJ_PIECES)]
        CONVERT_LAG = 6

        def slots(last):
            return range(SLOTS + (TAIL if last else 0))

        def unit_at(slot, lag, first):
            u = slot - lag
            return [u] if u < SLOTS and (u >= 0 or not first) else []

        def head_at(slot, lag, first):
            u = slot - lag - (TT - 1)
            return [u // TT] if u % TT == 0 and u < SLOTS and (u >= 0 or not first) else []

        def tile_at(slot, lag, first, last):
            k, odd = divmod(slot - lag - 1, 2)
            n = GROUP_TILES - TILES if last else GROUP_TILES
            return [k] if not odd and k < n and (k >= 0 or not first) else []

        def prep_at(slot, lag, last):
            return [c for c in range(CH) if PREP_FIRST + PREP_STEP * c + lag == slot and not last]

        def tile_place(k):
            return (k // TILES + 1) % 2, k % TILES

        def stage_pieces(wp_d, wg_d, wu_d, wd_d):
            pieces = []
            wp_v = wp_d.rearrange("(f p) n -> p f n", p=P)
            for i in range(4):
                pieces.append((wp_v[:, 8 * i:8 * i + 8], wp[:, 8 * i:8 * i + 8], 0.0))
            for k, src in enumerate((wg_d, wu_d)):
                v = src.rearrange("(c p) n -> p c n", p=P)
                for i in range(2):
                    pieces.append((v[:, 2 * i:2 * i + 2], wgu[:, 2 * i:2 * i + 2, k * HID:(k + 1) * HID], -128.0))
            v = wd_d.rearrange("(c p) n -> p c n", p=P)
            pieces.append((v[:, 0:6], wd[:, 0:6], -128.0))
            pieces.append((v[:, 6:HC], wd[:, 6:HC], -128.0))
            return pieces

        block = stack.enter_context(nc.Block())

        @block.sync
        def _(sp):
            for first in (x_loaded, heads_stored, *out_stored):
                sp.sem_inc(first, 16 * FREE)
            sp.dma_start(col[:], cols).then_inc(cols_in, 16)
            with sp.Fori(0, B) as b:
                sp.wait_ge(x_loaded, 16 * (b + FREE))
                x_dst = local[:, bass.ds((b % 2) * (2 * TT * DM), 2 * TT * DM)].bitcast(F32)
                sp.dma_start(x_dst.rearrange("p (t d) -> p t d", t=TT),
                             x_tiles[bass.ds(b, 1)].rearrange("o p t d -> (o p) t d")).then_inc(x_loaded, 16)
                sp.wait_ge(w_ready, b + FREE)
                sp.dma_start(w_raw[:], wg_chunks[0, bass.ds(b, 1)].rearrange("o p n -> (o p) n")).then_inc(w_loaded, 16)
                sp.wait_ge(ctx_lo_done, b + FREE)
                sp.dma_start(ctx_raw[:], ctx_chunks[bass.ds(b, 1)].rearrange("o p t -> (o p) t")).then_inc(ctx_loaded, 16)

            def stage_load(n):
                src, dst, _ = pieces[n]
                if n >= 2:
                    sp.wait_ge(stage_done, n - 1)
                rows, width = src.shape[1], src.shape[2]
                view = stage[:, n % 2, 0:rows * width].bitcast(src.dtype)
                sp.dma_start(view.rearrange("p (r w) -> p r w", w=width), src).then_inc(stage_loaded[n % 2], 16)

            pieces = stage_pieces(w_proj, w_gate, w_up, w_down)
            def group(g, first, last):
                for slot in slots(last):
                    for c in prep_at(slot, -PREP_FIRST, last):
                        sp.wait_ge(w_ready, CH * g + CH + c + FREE)
                        src = wg_chunks[bass.ds(g + 1, 1), c].rearrange("o p n -> (o p) n")
                        sp.dma_start(w_raw[:], src).then_inc(w_loaded, 16)
                    for H in head_at(slot, STORE_LAG, first):
                        if H % HEADS == HEADS - 1:
                            sp.wait_ge(heads_done, GROUP_HEADS * g + H + 1)
                            dst = heads_dram[H // HEADS % B, bass.ds(g + H // GROUP_HEADS, 1)]
                            sp.dma_start(dst.rearrange("o p n -> (o p) n"), heads.rearrange("p h t -> p (h t)"))\
                                .then_inc(heads_stored, 16)
                    if last and slot in STAGE_SLOTS:
                        if slot == STAGE_SLOTS[0]:
                            sp.wait_ge(proj_done, GROUP_TILES * G)
                        stage_load(STAGE_SLOTS.index(slot))

            group(0, True, False)
            with sp.Fori(1, G - 1) as g:
                group(g, False, False)

            group(G - 1, False, True)

            sp.wait_ge(heads_done, B * HEADS * G)
            sp.dma_start(sdown[:], s_down).then_inc(sdown_in, 16)
            sp.wait_ge(heads_stored, 16 * (B * G + FREE))
            sp.dma_start(heads_in.rearrange("p g h t -> p g (h t)"),
                         heads_dram[0].rearrange("g p n -> p g n")).then_inc(heads_back, 16)
            sp.dma_start(x_res[:], x_tiles[0]).then_inc(x_back, 16)
            for n in range(PROJ_PIECES, N_STAGE):
                stage_load(n)

            def store(b, tt):
                sp.wait_ge(out_ready, TT * b + tt + 1)
                dst = out_tiles[b, tt] if isinstance(b, int) else out_tiles[bass.ds(b, 1), tt].rearrange("o p d -> (o p) d")
                sp.dma_start(dst, y_out[:, tt % 2]).then_inc(out_stored[tt % 2], 16)

            with sp.Fori(1, B) as b:
                sp.wait_ge(pj_done, TT * b)
                sp.dma_start(heads_in.rearrange("p g h t -> p g (h t)"),
                             heads_dram[bass.ds(b, 1)].rearrange("o g p n -> p (o g) n")).then_inc(heads_back, 16)
                sp.wait_ge(x1_done, TT * b)
                sp.dma_start(x_res[:], x_tiles[bass.ds(b, 1)].rearrange("o p t d -> (o p) t d")).then_inc(x_back, 16)
                for tt in range(TT):
                    store(b - 1, tt)
            for tt in range(TT):
                store(B - 1, tt)
            for stored in out_stored:
                sp.wait_ge(stored, 16 * (B * TT // 2 + FREE))

        @block.tensor
        def _(pe):
            mm, tr = nc.tensor.matmul, nc.tensor.transpose
            pe.sem_inc(zt_done, FREE)
            pe.wait_ge(const_ready, 1)
            with pe.Fori(0, B) as b:
                pe.wait_ge(ln_z, 2 * b + 2)
                for c in range(CH):
                    if c >= 2:
                        pe.wait_ge(lnt_done, CH * b + c - 1)
                    for tt in range(TT):
                        last = tr(ps_pt[c % 2][:, tt * P:(tt + 1) * P], z2[:, tt, c * P:(c + 1) * P], ident[:])
                    last.then_inc(zt_done, 1)

            def w_at(par, part, c, at, n):
                start = part * PART + c * GW + at
                return w_bf[:, bass.ds(par * PAR + start, n)] if not isinstance(par, int) else \
                    w_bf[:, par * PAR + start:par * PAR + start + n]

            def project(b, i, half, par, t):
                c0 = i % TT
                tok = slice(b * T + c0 * P, b * T + (c0 + 1) * P)
                dst = ps_pj[i % 2]
                if half == 0 and not (isinstance(t, int) and t < 2):
                    pe.wait_ge(qn_done, t - 1)
                cross = i >= TT
                jobs = []
                if not cross:
                    jobs.append((0, 256, [(xq[:, 0, c, tok], c, part) for c in range(CH) for part in range(2)]))
                    jobs.append((256, 128, [(xq[:, 2, c, tok], c, part) for c in range(CH) for part in range(2)]))
                    jobs.append((384, 128, [(xq[:, 3, c, tok], c, part) for c in range(CH) for part in range(2)]))
                else:
                    jobs.append((0, 256, [(xq[:, 1, c, tok], c, part) for c in range(CH) for part in range(2)]))
                    jobs.append((256, 256, [(ctx_hi[:, c, tok], c, part) for c in range(CH) for part in range(2)] +
                                           [(ctx_lo[:, c, tok], c, 0) for c in range(CH)]))
                for at, n, terms in (jobs[:1] if half == 0 else jobs[1:]):
                    for k, (lhs, c, part) in enumerate(terms):
                        last = mm(dst[:, at:at + n], lhs, w_at(par, part, c, cross * 512 + at, n),
                                  start=(k == 0), stop=(k == len(terms) - 1))
                if half == 1:
                    last.then_inc(proj_done, 1)

            def turn_qk(i, t):
                pe.wait_ge(qn_done, t + 1)
                pe.wait_ge(full_done, t)
                for h in range(3):
                    last = tr(ps_qt[:, h * D:(h + 1) * D], qn[:, i % 2, h * D:(h + 1) * D], ident[:])
                last.then_inc(qt_done, 1)

            pe.wait_ge(w_ready, CH + FREE)
            pe.wait_ge(xq_done, B * CH)
            pe.wait_ge(ctx_lo_done, CH + FREE)
            for i in range(TILES):
                for half in range(2):
                    project(0, i, half, 0, i)
                if i >= 1:
                    turn_qk(i - 1, i - 1)
            turn_qk(TILES - 1, TILES - 1)

            def group(g, first, last):
                for slot in slots(last):
                    for u in unit_at(slot, 0, first):
                        b, head, qt = u // UNITS, u // TT % HEADS, u % TT
                        cross, hh = head // HPG, head % HPG
                        if u % (UNITS // 2) == 0:
                            pe.wait_ge(qklo_done, TILES * (B * g + b) + TT * (1 + cross))
                        if not first or u >= 2:
                            pe.wait_ge(exp_done, SLOTS * g + u - 1)
                        qs = slice(qt * P, (qt + 1) * P)
                        q_h, q_l = qk_hi[:, b % 2, cross, hh, qs], qk_lo[:, b % 2, cross, hh, qs]
                        k_h, k_l = qk_hi[:, b % 2, cross, 2], qk_lo[:, b % 2, cross, 2]
                        mm(ps_s[u % 2][:], q_h, k_h, start=True, stop=False)
                        mm(ps_s[u % 2][:], q_h, k_l, start=False, stop=False)
                        mm(ps_s[u % 2][:], q_l, k_h, start=False, stop=True).then_inc(s_done, 1)
                    for u in unit_at(slot, TURN_LAG, first):
                        pe.wait_ge(norm_done, SLOTS * g + u + 1)
                        if not first or u >= 2:
                            pe.wait_ge(ptlo_done, SLOTS * g + u - 1)
                        for tc in range(TT):
                            last_tr = tr(ps_pt[u % 2][:, tc * P:(tc + 1) * P], p_norm[:, u % 2, tc * P:(tc + 1) * P],
                                         ident[:])
                        last_tr.then_inc(pt_done, 1)
                    for k in tile_at(slot, QT_LAG, first, last):
                        turn_qk(tile_place(k)[1], GROUP_TILES * g + TILES + k)
                    for H in head_at(slot, PV_LAG, first):
                        b, head = H // HEADS, H % HEADS
                        cross = head // HPG
                        pe.wait_ge(ptlo_done, SLOTS * g + TT * (H + 1))
                        pe.wait_ge(y_done, GROUP_HEADS * g + H + FREE)
                        if head % HPG == 0:
                            pe.wait_ge(vlo_done, TILES * (B * g + b) + TT * (1 + cross))
                        for tc in range(TT):
                            vh, vl = v_hi[:, b % 2, cross, tc], v_lo[:, b % 2, cross, tc]
                            ph, pl = pt_hi[:, H % 2, tc], pt_lo[:, H % 2, tc]
                            mm(ps_o[:], vh, ph, start=(tc == 0), stop=False)
                            mm(ps_o[:], vh, pl, start=False, stop=False)
                            last_mm = mm(ps_o[:], vl, ph, start=False, stop=(tc == TT - 1))
                        last_mm.then_inc(pv_done, 1)
                    k, half = slot // 2, slot % 2
                    if k < (GROUP_TILES - TILES if last else GROUP_TILES):
                        b, i = k // TILES, k % TILES
                        if k == GROUP_TILES - TILES and half == 0:
                            pe.wait_ge(w_ready, CH * g + 2 * CH + FREE)
                        project((b + 1) % B, i, half, (g + 1) % 2 if b == B - 1 else g % 2, GROUP_TILES * g + TILES + k)

            group(0, True, False)
            with pe.Fori(1, G - 1) as g:
                group(g, False, False)
            group(G - 1, False, True)

            def out_projection(b):
                pe.wait_ge(heads_back, 16 * (b + 1))
                for tt in range(TT):
                    if tt >= 2:
                        pe.wait_ge(x1_done, TT * b + tt - 1)
                    for f in range(G * HEADS):
                        last = mm(ps_s[tt % 2][:], heads_in[:, f // HEADS, f % HEADS, tt * P:(tt + 1) * P], wp[:, f],
                                  start=(f == 0), stop=(f == G * HEADS - 1))
                    last.then_inc(pj_done, 1)

            def turn_z(b):
                pe.wait_ge(ln_z, 2 * B + b + 1)
                for tt in range(TT):
                    if tt >= 2:
                        pe.wait_ge(ztlo_done, TT * b + tt - 1)
                    for c in range(CH):
                        last = tr(ps_pt[tt % 2][:, c * P:(c + 1) * P], z3[:, tt, c * P:(c + 1) * P], ident[:])
                    last.then_inc(z3t_done, 1)

            def gate_up(b):
                pe.wait_ge(ztlo_done, TT * (b + 1))
                for m in range(HC):
                    for k, bank, signal in ((0, ps_pj[m % 2], gate_done), (1, ps_up[m % 2], up_done)):
                        if m >= 2:
                            pe.wait_ge(hid_done, HC * b + m - 1)
                        for c in range(CH):
                            w = wgu[:, c, k * HID + m * P:k * HID + (m + 1) * P]
                            mm(bank[:], w, zt_hi[:, c], start=(c == 0), stop=False)
                            last = mm(bank[:], w, zt_lo[:, c], start=False, stop=(c == CH - 1))
                        last.then_inc(signal, 1)

            def down(b, overlapped):
                pe.wait_ge(hlo_done, HC * (b + 1))
                for tt in range(TT):
                    if tt >= 2:
                        pe.wait_ge(scaled_done, TT * b + tt - 1)
                    elif overlapped:
                        pe.wait_ge(x1_done, TT * (b + 1) + tt + 3)
                    for m in range(HC):
                        ts = slice(tt * P, (tt + 1) * P)
                        mm(ps_s[tt % 2][:], h_hi[:, m, ts], wd[:, m], start=(m == 0), stop=False)
                        last = mm(ps_s[tt % 2][:], h_lo[:, m, ts], wd[:, m], start=False, stop=(m == HC - 1))
                    last.then_inc(down_done, 1)

            pe.wait_ge(stage_done, PROJ_PIECES)
            out_projection(0)
            turn_z(0)
            pe.wait_ge(stage_done, N_STAGE)
            gate_up(0)
            with pe.Fori(1, B) as b:
                out_projection(b)
                down(b - 1, True)
                turn_z(b)
                gate_up(b)
            down(B - 1, False)

        @block.scalar
        def _(act):
            a = nc.scalar.activation
            act.sem_inc(y_done, FREE)

            def weight_hi(par, c, count):
                act.wait_ge(w_scaled, count)
                act.sem_inc(waited_act, 1)
                a(w_bf[:, bass.ds(par * PAR + c * GW, GW)], w_raw[:], ACT.Copy).then_inc(w_hi_done, 1)

            act.wait_ge(scales_ready, 1)
            with act.Fori(0, B) as b:
                for c in range(CH):
                    act.wait_ge(lnt_done, CH * b + c + 1)
                    if c >= 2:
                        act.wait_ge(xq_done, CH * b + c - 1)
                    for s in range(SETS):
                        last = a(y4[:, c % 2, s * T:(s + 1) * T], ln_t[:, c % 2], ACT.Copy,
                                 scale=rscale[:, s * CH + c:s * CH + c + 1])
                    last.then_inc(y4_done, 1)
                weight_hi(0, b, b + 1)
                act.wait_ge(ctx_loaded, 16 * (b + 1))
                act.sem_inc(waited_act, 1)
                a(ctx_hi[:, bass.ds(b, 1)].rearrange("p o t -> p (o t)"), ctx_raw[:], ACT.Copy).then_inc(ctx_hi_done, 1)

            def squares(i, t):
                act.wait_ge(proj_done, t + 1)
                act.wait_ge(red_done, t)
                a(sq[:], ps_pj[i % 2][:, 0:3 * D], ACT.Square).then_inc(sq_done, 1)

            def v_part(b, i, t):
                a(v_hi[:, b % 2, i // TT, i % TT], ps_pj[i % 2][:, 3 * D:4 * D], ACT.Copy).then_inc(vhi_done, 1)

            def qk_part(b, i, t):
                act.wait_ge(qt_done, t + 1)
                act.wait_ge(qklo_done, t)
                cross, ts = i // TT, slice((i % TT) * P, (i % TT + 1) * P)
                w, bias = qscaled[:, 2 * cross:2 * cross + 1], qscaled[:, 2 * cross + 1:2 * cross + 2]
                kw, kb = ("kxln_w", "kxln_b") if cross else ("kln_w", "kln_b")
                q_in, k_in = ps_qt[:, 0:2 * D], ps_qt[:, 2 * D:3 * D]
                a(qk_hi[:, b % 2, cross, 0:2, ts], q_in.rearrange("p (h t) -> p h t", h=2), ACT.Identity, bias=bias, scale=w)
                a(qk_hi[:, b % 2, cross, 2, ts], k_in, ACT.Identity, bias=c_(kb), scale=c_(kw))
                a(qk_full[:, 0:2 * D], q_in, ACT.Identity, bias=bias, scale=w)
                a(qk_full[:, 2 * D:3 * D], k_in, ACT.Identity, bias=c_(kb), scale=c_(kw)).then_inc(full_done, 1)

            act.wait_ge(xq_done, B * CH)
            for i in range(TILES):
                squares(i, i)
                v_part(0, i, i)
                if i >= 1:
                    qk_part(0, i - 1, i - 1)
            qk_part(0, TILES - 1, TILES - 1)

            def convert(n):
                src, dst, offset = stage_pieces(w_proj, w_gate, w_up, w_down)[n]
                act.wait_ge(stage_loaded[n % 2], 16 * (n // 2 + 1))
                rows, width = src.shape[1], src.shape[2]
                raw = stage[:, n % 2, 0:rows * width].bitcast(src.dtype).rearrange("p (r w) -> p r w", w=width)
                a(dst, raw, ACT.Copy, bias=offset).then_inc(stage_done, 1)

            def group(g, first, last):
                for slot in slots(last):
                    for u in unit_at(slot, EXP_LAG, first):
                        act.wait_ge(max_done, SLOTS * g + u + 1)
                        if not first or u >= 2:
                            act.wait_ge(norm_done, SLOTS * g + u - 1)
                        a(p_exp[:, u % 2], ps_s[u % 2][:], ACT.Exp, bias=neg_max[:, u % 4:u % 4 + 1],
                          accum_out=p_sum[:, u % 4:u % 4 + 1]).then_inc(exp_done, 1)
                    for k in tile_at(slot, SQ_LAG, first, last):
                        b, i = tile_place(k)
                        t = GROUP_TILES * g + TILES + k
                        squares(i, t)
                        v_part(b, i, t)
                    for k in tile_at(slot, QK_LAG, first, last):
                        qk_part(*tile_place(k), GROUP_TILES * g + TILES + k)
                    for u in unit_at(slot, TURN_LAG, first):
                        H, qt = u // TT, u % TT
                        act.wait_ge(pt_done, SLOTS * g + u + 1)
                        if qt == 0 and (not first or H >= 2):
                            act.wait_ge(pv_done, GROUP_HEADS * g + H - 1)
                        a(pt_hi[:, H % 2, :, qt * P:(qt + 1) * P], ps_pt[u % 2].rearrange("p (c t) -> p c t", c=TT),
                          ACT.Copy).then_inc(pthi_done, 1)
                    for c in prep_at(slot, HI_LAG, last):
                        weight_hi((g + 1) % 2, c, CH * g + CH + c + 1)
                    for H in head_at(slot, Y_LAG, first):
                        act.wait_ge(pv_done, GROUP_HEADS * g + H + 1)
                        if not first or H >= 2:
                            act.wait_ge(heads_done, GROUP_HEADS * g + H - 1)
                        act.sem_inc(waited_act, 1)
                        column = HEADS * (g + H // GROUP_HEADS) + H % HEADS
                        a(y[:, H % 2], ps_o[:], ACT.Copy, scale=rsmooth[:, bass.ds(column, 1)]).then_inc(y_done, 1)
                    if last and slot - CONVERT_LAG in STAGE_SLOTS:
                        convert(STAGE_SLOTS.index(slot - CONVERT_LAG))

            group(0, True, False)
            with act.Fori(1, G - 1) as g:
                group(g, False, False)
            group(G - 1, False, True)
            for n in range(PROJ_PIECES, N_STAGE):
                convert(n)

            def finish(b):
                for tt in range(TT):
                    act.wait_ge(z3t_done, TT * b + tt + 1)
                    a(zt_hi[:, :, tt * P:(tt + 1) * P], ps_pt[tt % 2].rearrange("p (c t) -> p c t", c=CH), ACT.Copy)\
                        .then_inc(zthi_done, 1)

                def h_part(m):
                    act.wait_ge(hid_done, HC * b + m + 1)
                    a(h_hi[:, m], hid[:, m % 2], ACT.Copy).then_inc(hhi_done, 1)

                for m in range(HC):
                    act.wait_ge(gate_done, HC * b + m + 1)
                    if m >= 2:
                        act.wait_ge(hid_done, HC * b + m - 1)
                    a(silu[:, m % 2], ps_pj[m % 2][:], ACT.Silu, scale=c_("s_gate", m)).then_inc(silu_done, 1)
                    if m >= 1:
                        h_part(m - 1)
                h_part(HC - 1)

            with act.Fori(0, B) as b:
                finish(b)

        @block.gpsimd
        def _(pool):
            nc.gpsimd.memset(ident[:], 0.0).then_inc(ident_zero, 1)
            pool.wait_ge(ident_zero, 1)
            nc.gpsimd.affine_select(out=ident[:], in_=ident[:], compare_op=ALU.not_equal, fill=1.0, base=0,
                                    pattern=[[-1, P]], channel_multiplier=1).then_inc(const_ready, 1)
            nc.gpsimd.memset(minus_half[:], -0.5).then_inc(const_ready, 1)
            tt_ = nc.gpsimd.tensor_tensor

            def spread_cols(v):
                return v.unsqueeze(2).to_broadcast([P, 8, D])

            w3 = w_raw[:].rearrange("p (k d) -> p k d", k=8)

            def weight_centre(count):
                pool.wait_ge(w_step, 2 * count)
                tt_(w3, w3, spread_cols(w_mean[:]), ALU.subtract).then_inc(w_centred, 1)

            def weight_scale(c, count):
                pool.wait_ge(w_centred, count)
                tt_(w3, w3, spread_cols(wscale[:, bass.ds(8 * c, 8)]), ALU.mult).then_inc(w_scaled, 1)

            def power(n):
                pool.wait_ge(ln_var, n + 1)
                tt_(rstd[:], spread[:], minus_half[:, 0:TT], ALU.pow).then_inc(ln_rstd, 1)

            pool.wait_ge(const_ready, 2)
            pool.wait_ge(scales_ready, 1)
            with pool.Fori(0, B) as b:
                power(2 * b)
                power(2 * b + 1)
                weight_centre(b + 1)
                weight_scale(b, b + 1)

            def head_power(i, t):
                pool.wait_ge(var_done, t + 1)
                tt_(head_rstd[:, i % 2, 0:3], head_var[:, i % 2, 0:3], minus_half[:, 0:3], ALU.pow).then_inc(rstd_done, 1)

            def qk_rest(b, i, t):
                pool.wait_ge(full_done, t + 1)
                cross, ts = i // TT, slice((i % TT) * P, (i % TT + 1) * P)
                tt_(qk_lo[:, b % 2, cross, :, ts], qk_full[:].rearrange("p (h t) -> p h t", h=3),
                    qk_hi[:, b % 2, cross, :, ts], ALU.subtract).then_inc(qklo_done, 1)

            for i in range(TILES):
                head_power(i, i)
                if i >= 1:
                    qk_rest(0, i - 1, i - 1)
            qk_rest(0, TILES - 1, TILES - 1)

            def group(g, first, last):
                for slot in slots(last):
                    for k in tile_at(slot, REST_LAG, first, last):
                        qk_rest(*tile_place(k), GROUP_TILES * g + TILES + k)
                    for u in unit_at(slot, EXP_LAG, first):
                        pool.wait_ge(rsum_done, SLOTS * g + u + 1)
                        if not first or u >= 2:
                            pool.wait_ge(pt_done, SLOTS * g + u - 1)
                        tt_(p_norm[:, u % 2], p_exp[:, u % 2], r_sum[:, u % 4:u % 4 + 1].to_broadcast([P, T]), ALU.mult)\
                            .then_inc(norm_done, 1)
                    for k in tile_at(slot, VAR_LAG, first, last):
                        head_power(tile_place(k)[1], GROUP_TILES * g + TILES + k)
                    for c in prep_at(slot, CENTRE_LAG, last):
                        weight_centre(CH * g + CH + c + 1)
                    for c in prep_at(slot, SCALE_LAG, last):
                        weight_scale(c, CH * g + CH + c + 1)

            group(0, True, False)
            with pool.Fori(1, G - 1) as g:
                group(g, False, False)
            group(G - 1, False, True)

            with pool.Fori(0, B) as b:
                power(2 * B + b)
                for m in range(HC):
                    pool.wait_ge(hhi_done, HC * b + m + 1)
                    tt_(h_lo[:, m], hid[:, m % 2], h_hi[:, m], ALU.subtract).then_inc(hlo_done, 1)

        @block.vector
        def _(dve):
            v = nc.vector
            dve.sem_inc(w_ready, FREE)
            dve.sem_inc(ctx_lo_done, FREE)
            v.memset(centre[:], 1.0 / D).then_inc(ones_set, 1)
            dve.wait_ge(ones_set, 1)
            dve.wait_ge(cols_in, 16)
            v.reciprocal(rscale[:], c_("in_scale", 0, SETS * CH))
            v.reciprocal(rsmooth[:], c_("smooth", 0, NH * 2))
            v.tensor_tensor(pscale[:], c_("proj_in"), c_("proj_w"), ALU.mult)
            for k, name in enumerate(("qln_w", "qln_b", "qxln_w", "qxln_b")):
                v.tensor_scalar(qscaled[:, k:k + 1], c_(name), float(D) ** -0.5, None, ALU.mult)
            v.memset(centre[:, 3:4], 0.0)
            v.memset(centre[:, 7:8], 0.0)
            v.memset(wscale[:], 1.0).then_inc(ones_set, 1)
            dve.wait_ge(ones_set, 2)
            for k, s in ((0, 0), (1, 0), (2, 2), (3, 3), (4, 1), (5, 1)):
                last = v.tensor_scalar(wscale[:].rearrange("p (c k) -> p c k", k=8)[:, :, k], c_("in_scale", s * CH, CH), c_("w_scale", s), None, ALU.mult)
            last.then_inc(scales_ready, 1)
            dve.wait_ge(scales_ready, 1)

            def weight_sums(count):
                dve.wait_ge(w_loaded, 16 * count)
                v.tensor_reduce(w_sum[:], w_raw[:].rearrange("p (k d) -> p k d", k=8), AX_X, ALU.add).then_inc(w_step, 1)
                dve.wait_ge(w_step, 2 * count - 1)
                v.tensor_tensor(w_mean[:], w_sum[:], centre[:], ALU.mult).then_inc(w_step, 1)

            def weight_lo(par, c, count):
                dve.wait_ge(w_hi_done, count)
                hi = w_bf[:, bass.ds(par * PAR + c * GW, GW)]
                lo = w_bf[:, bass.ds(par * PAR + c * GW + PART, GW)]
                v.tensor_tensor(lo, w_raw[:], hi, ALU.subtract).then_inc(w_ready, 1)

            def layer_norm(n, src, dst):
                for tt in range(TT):
                    v.bn_stats(stats[:, tt], src(tt)).then_inc(ln_step, 1)
                dve.wait_ge(ln_step, LN_STEPS * n + TT)
                dve.sem_inc(waited_dve, 1)
                for tt in range(TT):
                    v.bn_aggr(moments[:, tt], stats[:, tt]).then_inc(ln_step, 1)
                dve.wait_ge(ln_step, LN_STEPS * (n + 1))
                v.tensor_scalar(spread[:], moments[:, :, 1], EPS, None, ALU.add).then_inc(ln_var, 1)
                dve.wait_ge(ln_rstd, n + 1)
                for tt in range(TT):
                    last = v.tensor_scalar(dst[:, tt], src(tt), moments[:, tt, 0:1], rstd[:, tt:tt + 1],
                                           ALU.subtract, ALU.mult)
                last.then_inc(ln_z, 1)

            def quantise(n, dst, val, magnitude, total, signal, free=None):
                at = QUANT_STEPS * n
                v.tensor_scalar(val, val, FP8_MAX, -FP8_MAX, ALU.min, ALU.max).then_inc(quant_step, 1)
                dve.wait_ge(quant_step, at + 1)
                v.tensor_scalar(magnitude.bitcast(I16), val.bitcast(I16), EXPONENT, None, ALU.bitwise_and)\
                    .then_inc(quant_step, 1)
                dve.wait_ge(quant_step, at + 2)
                v.tensor_scalar(magnitude, magnitude, MIN_BINADE, KEEP4, ALU.max, ALU.mult).then_inc(quant_step, 1)
                dve.wait_ge(quant_step, at + 3)
                v.tensor_tensor(total, val, magnitude, ALU.add).then_inc(quant_step, 1)
                dve.wait_ge(quant_step, at + 4)
                if free:
                    free()
                shape = dst.shape
                if len(shape) == 3:
                    total = total.rearrange("p (s t) -> p s t", t=shape[2])
                    magnitude = magnitude.rearrange("p (s t) -> p s t", t=shape[2])
                v.tensor_tensor(dst, total, magnitude, ALU.subtract).then_inc(signal, 1)

            with dve.Fori(0, B) as b:
                dve.wait_ge(x_loaded, 16 * (b + 1 + FREE))
                dve.sem_inc(waited_dve, 1)
                xb = local[:, bass.ds((b % 2) * (2 * TT * DM), 2 * TT * DM)].bitcast(F32)
                layer_norm(2 * b, lambda tt: xb[:, tt * DM:(tt + 1) * DM], z1)
                dve.wait_ge(ln_z, 2 * b + 1)
                dve.wait_ge(zt_done, CH * b + FREE)
                dve.sem_inc(waited_dve, 1)
                layer_norm(2 * b + 1, lambda tt: z1[:, tt], z2)

                def quantise_chunk(c):
                    dve.wait_ge(y4_done, CH * b + c + 1)
                    quantise(CH * b + c, xq[:, :, c, bass.ds(b * T, T)], y4[:, c % 2], mag4, sum4, xq_done)

                for c in range(CH):
                    dve.wait_ge(zt_done, CH * b + c + 1 + FREE)
                    if c >= 2:
                        dve.wait_ge(y4_done, CH * b + c - 1)
                    v.tensor_scalar(ln_t[:, c % 2], ps_pt[c % 2][:], c_("ln_w", c), c_("ln_b", c), ALU.mult, ALU.add)\
                        .then_inc(lnt_done, 1)
                    if c >= 1:
                        quantise_chunk(c - 1)
                quantise_chunk(CH - 1)
                weight_sums(b + 1)
                weight_lo(0, b, b + 1)
                dve.wait_ge(ctx_hi_done, b + 1)
                v.tensor_tensor(ctx_lo[:, bass.ds(b, 1)].rearrange("p o t -> p (o t)"), ctx_raw[:],
                                ctx_hi[:, bass.ds(b, 1)].rearrange("p o t -> p (o t)"), ALU.subtract).then_inc(ctx_lo_done, 1)

            def head_variance(i, t):
                dve.wait_ge(sq_done, t + 1)
                v.tensor_reduce(sq_sum[:, i % 2, 0:3], sq[:].rearrange("p (h d) -> p h d", h=3), AX_X, ALU.add)\
                    .then_inc(red_done, 1)
                dve.wait_ge(red_done, t + 1)
                v.tensor_scalar(head_var[:, i % 2, 0:3], sq_sum[:, i % 2, 0:3], 1.0 / D, EPS, ALU.mult, ALU.add)\
                    .then_inc(var_done, 1)

            def v_rest(b, i, t):
                dve.wait_ge(vhi_done, t + 1)
                v.tensor_tensor(v_lo[:, b % 2, i // TT, i % TT], ps_pj[i % 2][:, 3 * D:4 * D],
                                v_hi[:, b % 2, i // TT, i % TT], ALU.subtract).then_inc(vlo_done, 1)

            def head_norm(i, t):
                dve.wait_ge(rstd_done, t + 1)
                if not isinstance(t, int) or t >= 2:
                    dve.wait_ge(qt_done, t - 1)
                v.tensor_tensor(qn[:, i % 2].rearrange("p (h d) -> p h d", h=3),
                                ps_pj[i % 2][:, 0:3 * D].rearrange("p (h d) -> p h d", h=3),
                                head_rstd[:, i % 2, 0:3].unsqueeze(2).to_broadcast([P, 3, D]), ALU.mult)\
                    .then_inc(qn_done, 1)

            for i in range(TILES):
                head_variance(i, i)
                v_rest(0, i, i)
                head_norm(i, i)

            def group(g, first, last):
                for slot in slots(last):
                    for u in unit_at(slot, SPLIT_LAG, first):
                        H, qt = u // TT, u % TT
                        dve.wait_ge(pthi_done, SLOTS * g + u + 1)
                        dst = slice(qt * P, (qt + 1) * P)
                        v.tensor_tensor(pt_lo[:, H % 2, :, dst], ps_pt[u % 2].rearrange("p (c t) -> p c t", c=TT),
                                        pt_hi[:, H % 2, :, dst], ALU.subtract).then_inc(ptlo_done, 1)
                    for u in unit_at(slot, 0, first):
                        dve.wait_ge(s_done, SLOTS * g + u + 1)
                        v.tensor_reduce(neg_max[:, u % 4:u % 4 + 1], ps_s[u % 2][:], AX_X, ALU.max, negate=True)\
                            .then_inc(max_done, 1)
                    for u in unit_at(slot, EXP_LAG, first):
                        dve.wait_ge(exp_done, SLOTS * g + u + 1)
                        v.reciprocal(r_sum[:, u % 4:u % 4 + 1], p_sum[:, u % 4:u % 4 + 1]).then_inc(rsum_done, 1)
                    for k in tile_at(slot, QN_LAG, first, last):
                        head_norm(tile_place(k)[1], GROUP_TILES * g + TILES + k)
                    for k in tile_at(slot, VAR_LAG, first, last):
                        b, i = tile_place(k)
                        head_variance(i, GROUP_TILES * g + TILES + k)
                        v_rest(b, i, GROUP_TILES * g + TILES + k)
                    for c in prep_at(slot, 0, last):
                        weight_sums(CH * g + CH + c + 1)
                    for c in prep_at(slot, LO_LAG, last):
                        weight_lo((g + 1) % 2, c, CH * g + CH + c + 1)
                    for H in head_at(slot, QUANT_LAG, first):
                        head = H % HEADS
                        dve.wait_ge(y_done, GROUP_HEADS * g + H + 1 + FREE)

                        def stored():
                            if head == 0:
                                dve.wait_ge(heads_stored, 16 * (B * g + H // HEADS + FREE))
                        quantise(B * CH + GROUP_HEADS * g + H, heads[:, head], y[:, H % 2], mag, summed, heads_done, stored)

            group(0, True, False)
            with dve.Fori(1, G - 1) as g:
                group(g, False, False)
            group(G - 1, False, True)

            def x1_at(b, tt):
                if isinstance(b, int):
                    at = (b % 2) * TT * DM + tt * DM
                    return x1[:, at:at + DM]
                return x1[:, bass.ds((b % 2) * (TT * DM) + tt * DM, DM)]

            def residual(b):
                dve.wait_ge(x_back, 16 * (b + 1))
                for tt in range(TT):
                    dve.wait_ge(pj_done, TT * b + tt + 1)
                    v.scalar_tensor_tensor(x1_at(b, tt), ps_s[tt % 2][:], pscale[:, 0:1], x_res[:, tt], ALU.mult, ALU.add)\
                        .then_inc(x1_done, 1)
                dve.wait_ge(x1_done, TT * (b + 1))
                dve.sem_inc(waited_dve, 1)
                layer_norm(2 * B + b, lambda tt: x1_at(b, tt), z3)

            def output(b):
                for tt in range(TT):
                    dve.wait_ge(down_done, TT * b + tt + 1)
                    v.tensor_tensor(scaled[:, tt % 2], ps_s[tt % 2][:], sdown[:], ALU.mult).then_inc(scaled_done, 1)
                    dve.wait_ge(scaled_done, TT * b + tt + 1)
                    dve.wait_ge(out_stored[tt % 2], 16 * (TT // 2 * b + tt // 2 + FREE))
                    v.tensor_tensor(y_out[:, tt % 2], scaled[:, tt % 2], x1_at(b, tt), ALU.add).then_inc(out_ready, 1)

            def hidden(b):
                for tt in range(TT):
                    dve.wait_ge(zthi_done, TT * b + tt + 1)
                    dst = slice(tt * P, (tt + 1) * P)
                    v.tensor_tensor(zt_lo[:, :, dst], ps_pt[tt % 2].rearrange("p (c t) -> p c t", c=CH), zt_hi[:, :, dst],
                                    ALU.subtract).then_inc(ztlo_done, 1)
                for m in range(HC):
                    dve.wait_ge(silu_done, HC * b + m + 1)
                    dve.wait_ge(up_done, HC * b + m + 1)
                    if m >= 2:
                        dve.wait_ge(hlo_done, HC * b + m - 1)
                    v.scalar_tensor_tensor(hid[:, m % 2], ps_up[m % 2][:], c_("s_up", m), silu[:, m % 2],
                                           ALU.mult, ALU.mult).then_inc(hid_done, 1)

            dve.wait_ge(sdown_in, 16)
            residual(0)
            hidden(0)
            with dve.Fori(1, B) as b:
                residual(b)
                output(b - 1)
                hidden(b)
            output(B - 1)


def kernel(**inputs):
    import concourse.bacc as bacc
    from concourse.bass_utils import run_bass_kernel_spmd

    a = {k: np.asarray(v) for k, v in inputs.items()}
    xa = {k[len("L0_xattn_"):]: v for k, v in a.items() if k.startswith("L0_xattn_")}
    ff = {k[len("L0_ffn_"):]: v for k, v in a.items() if k.startswith("L0_ffn_")}

    def per_group(w, n):
        return w.reshape(G, n, DM).transpose(0, 2, 1)

    kvx = xa["w_kv_x"]
    w_group = np.concatenate([per_group(xa["wq"], 256), per_group(xa["wk"], 128), per_group(xa["wv"], 128),
                              per_group(xa["wqx"], 256), per_group(kvx[:G * D], 128), per_group(kvx[G * D:], 128)], axis=2)
    order = [f for g in range(G) for f in (2 * g, 2 * g + 1, NH + 2 * g, NH + 2 * g + 1)]
    w_proj = xa["wproj"].T.reshape(2 * NH, D, DM)[order].reshape(2 * NH * D, DM)
    smooth = xa["proj_smooth"].reshape(2 * NH, D)[order]

    def column(v):
        return np.broadcast_to(v.reshape(1, 1), (P, 1))

    def chunked(v):
        return v.reshape(-1, P).T

    parts = {
        "ln_w": chunked(xa["ln_w"]), "ln_b": chunked(xa["ln_b"]),
        "in_scale": np.concatenate([chunked(xa[f"{n}_in_scale"]) for n in ("q", "qx", "k", "v")], axis=1),
        "w_scale": np.concatenate([column(xa[f"w{n}_scale"]) for n in ("q", "qx", "k", "v")], axis=1),
        **{n: chunked(xa[n]) for n in ("qln_w", "qln_b", "qxln_w", "qxln_b", "kln_w", "kln_b", "kxln_w", "kxln_b")},
        "smooth": smooth.T, "s_gate": chunked(ff["s_gate"]), "s_up": chunked(ff["s_up"]),
        "proj_in": column(xa["proj_in_scale"]), "proj_w": column(xa["proj_w_scale"]),
    }
    arrays = {
        "x": a["x"].reshape(NTOK, DM),
        "ctx_t": a["ctx_2048"].reshape(NTOK, DM).T,
        "w_group": w_group,
        "w_proj": w_proj,
        "w_gate": ff["wq_gate"].T,
        "w_up": ff["wq_up"].T,
        "w_down": ff["wq_down"].T,
        "cols": np.concatenate([parts[n] for n in COLS], axis=1),
        "s_down": np.broadcast_to(ff["s_down"].reshape(1, DM), (P, DM)),
    }
    arrays = {k: np.ascontiguousarray(v) for k, v in arrays.items()}

    nc = bacc.Bacc("TRN2", target_bir_lowering=False, num_devices=1)
    args = [nc.dram_tensor(n, v.shape, mybir.dt.from_np(v.dtype), kind="ExternalInput").ap() for n, v in arrays.items()]
    out = nc.dram_tensor("out", (NTOK, DM), F32, kind="ExternalOutput").ap()
    block_kernel(nc, *args, out)
    r = run_bass_kernel_spmd(nc, [arrays], core_ids=[0])
    return r.results[0]["out"].reshape(B, T, DM)
```

```python
from contextlib import ExitStack

import numpy as np

import concourse.bass as bass
from concourse import mybir

F32 = mybir.dt.float32
BF16 = mybir.dt.bfloat16
I16 = mybir.dt.int16
I32 = mybir.dt.int32
ALU = mybir.AluOpType
ACT = mybir.ActivationFunctionType
AX_X = mybir.AxisListType.X

P = 128
B, T, DM = 4, 512, 512
NTOK = B * T
G, D = 8, 128
HPG = 2
NH = G * HPG
CH = DM // P
TT = T // P
HID = 1408
HC = HID // P
SETS = 4
GW = 8 * D
HEADS = 2 * HPG
UNITS = HEADS * TT
TILES = 2 * TT
EPS = 1e-5
FP8_MAX = 448.0
EXPONENT = 0x7F80
MIN_BINADE = 2.0 ** -6
KEEP4 = 24.0

FREE = 1
W_FREE = 2
Z_FREE = 2 * 2

COLS = {}
for _name, _n in (("ln_w", CH), ("ln_b", CH), ("in_scale", SETS * CH), ("w_scale", SETS), ("qln_w", 1), ("qln_b", 1),
                  ("qxln_w", 1), ("qxln_b", 1), ("kln_w", 1), ("kln_b", 1), ("kxln_w", 1), ("kxln_b", 1),
                  ("smooth", NH * 2), ("s_gate", HC), ("s_up", HC), ("proj_in", 1), ("proj_w", 1)):
    COLS[_name] = (sum(n for _, n in COLS.values()), _n)
NCOLS = sum(n for _, n in COLS.values())


def block_kernel(nc, x, ctx_t, w_group, w_proj, w_gate, w_up, w_down, cols, s_down, out):
    x_tiles = x.rearrange("(b t p) d -> b p t d", b=B, p=P)
    out_tiles = out.rearrange("(b t p) d -> b t p d", b=B, p=P)
    ctx_chunks = ctx_t.rearrange("(c p) t -> c p t", p=P)
    wg_chunks = w_group.rearrange("g (c p) n -> g c p n", p=P)
    heads_dram = nc.dram_tensor("quantised_heads", (B, G, P, HEADS * T), BF16, kind="Internal").ap()

    stack = ExitStack()
    with stack:
        def sb(name, shape, dt):
            return stack.enter_context(nc.sbuf_tensor(name, shape, dt))

        def psum(name):
            return stack.enter_context(nc.psum_tensor(name, [P, 512], F32))

        def sem(name):
            return stack.enter_context(nc.semaphore(name))

        wide = sb("wide", [P, 65536], BF16)
        local = sb("local", [P, 35840], BF16)
        w_raw = sb("w_raw", [P, 2 * GW], F32)
        ident = sb("ident", [P, P], F32)
        col = sb("col", [P, NCOLS], F32)
        wscale = sb("wscale", [P, CH * 8], F32)
        rsmooth = sb("rsmooth", [P, NH * 2], F32)
        qscaled = sb("qscaled", [P, 4], F32)
        pscale = sb("pscale", [P, 1], F32)
        centre = sb("centre", [P, 8], F32)
        minus_half = sb("minus_half", [P, 8], F32)
        stats = sb("stats", [P, TT, 6], F32)
        moments = sb("moments", [P, TT, 2], F32)
        spread = sb("spread", [P, TT], F32)
        rstd = sb("rstd", [P, TT], F32)
        w_sum = sb("w_sum", [P, 8], F32)
        w_mean = sb("w_mean", [P, 8], F32)
        neg_max = sb("neg_max", [P, 4], F32)
        p_sum = sb("p_sum", [P, 4], F32)
        r_sum = sb("r_sum", [P, 4], F32)
        sq_sum = sb("sq_sum", [P, 2, 4], F32)
        head_var = sb("head_var", [P, 2, 4], F32)
        head_rstd = sb("head_rstd", [P, 2, 4], F32)

        class Carve:
            def __init__(self, region):
                self.region, self.at = region, 0

            def __call__(self, shape, dt):
                n = int(np.prod(shape)) * (2 if dt in (F32, I32) else 1)
                v = self.region[:, self.at:self.at + n]
                self.at += n
                if dt != BF16:
                    v = v.bitcast(dt)
                if len(shape) == 1:
                    return v
                names = "abcde"[:len(shape)]
                return v.rearrange(f"p ({' '.join(names)}) -> p {' '.join(names)}",
                                   **{k: s for k, s in zip(names[1:], shape[1:])})

        def c_(name, i=0, n=1):
            at = COLS[name][0] + i
            return col[:, at:at + n]

        carve = Carve(wide)
        xq = carve([SETS, CH, NTOK], BF16)
        ctx_hi = carve([CH, NTOK], BF16)
        ctx_lo = carve([CH, NTOK], BF16)
        PART, PAR = CH * GW, 2 * CH * GW
        w_bf = carve([2 * PAR], BF16)
        carve = Carve(wide)
        wp = carve([G * HEADS, DM], BF16)
        wgu = carve([CH, 2 * HID], BF16)
        wd = carve([HC, DM], BF16)
        stage = carve([2, 4096], F32)
        h_hi = carve([HC, T], BF16)
        h_lo = carve([HC, T], BF16)
        zt_hi = carve([CH, T], BF16)
        zt_lo = carve([CH, T], BF16)
        carve = Carve(stage.rearrange("p a b -> p (a b)").bitcast(BF16))
        silu = carve([2, T], F32)
        hid = carve([2, T], F32)
        scaled = carve([2, DM], F32)
        carve = Carve(local)
        x_in = carve([2, TT, DM], F32)
        z1 = carve([TT, DM], F32)
        z2 = carve([TT, DM], F32)
        y4 = carve([2, SETS * T], BF16)
        mag4 = carve([SETS * T], BF16)
        sum4 = carve([SETS * T], BF16)
        ctx_raw = carve([NTOK], F32)
        rscale = carve([SETS * CH], F32)
        ln_scale = carve([SETS * CH], F32)
        ln_bias = carve([SETS * CH], F32)
        carve = Carve(local)
        qk_hi = carve([2, 2, 3, T], BF16)
        qk_lo = carve([2, 2, 3, T], BF16)
        v_hi = carve([2, 2, TT, D], BF16)
        v_lo = carve([2, 2, TT, D], BF16)
        pt_hi = carve([2, TT, T], BF16)
        pt_lo = carve([2, TT, T], BF16)
        heads = carve([HEADS, T], BF16)
        y = carve([2, T], BF16)
        mag = carve([T], BF16)
        summed = carve([T], BF16)
        sq = carve([3 * D], F32)
        qn = carve([2, 3 * D], F32)
        qk_full = carve([3 * D], F32)
        p_exp = carve([2, T], F32)
        p_norm = carve([2, T], F32)
        carve = Carve(local)
        heads_in = carve([G, HEADS, T], BF16)
        x1 = carve([2 * TT * DM], F32)
        x_res = carve([TT, DM], F32)
        z3 = carve([TT, DM], F32)
        y_out = carve([2, DM], F32)
        sdown = carve([DM], F32)

        ps_s = [psum(f"ps_s{i}") for i in range(2)]
        ps_pt = [psum(f"ps_pt{i}") for i in range(2)]
        ps_pj = [psum(f"ps_pj{i}") for i in range(2)]
        ps_qt = psum("ps_qt")
        ps_o = psum("ps_o")
        ps_up = [ps_qt, ps_o]

        def raw(c):
            return w_raw[:, bass.ds((c % 2) * GW, GW)]

        waited_act = sem("waited_act")
        waited_dve = sem("waited_dve")
        cols_in = sem("cols_in")
        ident_zero = sem("ident_zero")
        ones_set = sem("ones_set")
        const_ready = sem("const_ready")
        scales_ready = sem("scales_ready")
        x_loaded = sem("x_loaded")
        ctx_loaded = sem("ctx_loaded")
        ctx_hi_done = sem("ctx_hi_done")
        ctx_lo_done = sem("ctx_lo_done")
        ln_step = sem("ln_step")
        ln_var = sem("ln_var")
        ln_rstd = sem("ln_rstd")
        ln_z = sem("ln_z")
        zt_done = sem("zt_done")
        y4_done = sem("y4_done")
        quant_step = sem("quant_step")
        xq_done = sem("xq_done")
        w_loaded = sem("w_loaded")
        w_step = sem("w_step")
        w_centred = sem("w_centred")
        w_scaled = sem("w_scaled")
        w_hi_done = sem("w_hi_done")
        w_ready = sem("w_ready")
        proj_done = sem("proj_done")
        sq_done = sem("sq_done")
        vhi_done = sem("vhi_done")
        vlo_done = sem("vlo_done")
        red_done = sem("red_done")
        var_done = sem("var_done")
        rstd_done = sem("rstd_done")
        qn_done = sem("qn_done")
        qt_done = sem("qt_done")
        full_done = sem("full_done")
        qklo_done = sem("qklo_done")
        s_done = sem("s_done")
        max_done = sem("max_done")
        exp_done = sem("exp_done")
        rsum_done = sem("rsum_done")
        norm_done = sem("norm_done")
        pt_done = sem("pt_done")
        pthi_done = sem("pthi_done")
        ptlo_done = sem("ptlo_done")
        pv_done = sem("pv_done")
        y_done = sem("y_done")
        heads_done = sem("heads_done")
        heads_stored = sem("heads_stored")
        stage_loaded = [sem(f"stage_loaded{i}") for i in range(2)]
        stage_done = sem("stage_done")
        sdown_in = sem("sdown_in")
        heads_back = sem("heads_back")
        x_back = sem("x_back")
        pj_done = sem("pj_done")
        x1_done = sem("x1_done")
        z3t_done = sem("z3t_done")
        zthi_done = sem("zthi_done")
        ztlo_done = sem("ztlo_done")
        gate_done = sem("gate_done")
        up_done = sem("up_done")
        silu_done = sem("silu_done")
        hid_done = sem("hid_done")
        hhi_done = sem("hhi_done")
        hlo_done = sem("hlo_done")
        down_done = sem("down_done")
        scaled_done = sem("scaled_done")
        out_ready = sem("out_ready")
        out_stored = [sem(f"out_stored{i}") for i in range(2)]

        LN_STEPS = 2 * TT
        QUANT_STEPS = 4
        N_STAGE, PROJ_PIECES, GATE_UP_PIECES = 10, 4, 4

        SLOTS = B * UNITS
        GROUP_TILES = B * TILES
        GROUP_HEADS = B * HEADS
        MAX_LAG, EXP_LAG, SUM_LAG, NORM_LAG = 1, 1, 2, 2
        TURN_LAG, HI_LAG, LO_LAG = 3, 4, 4
        PV_LAG, Y_LAG, QUANT_LAG, STORE_LAG = 6, 9, 10, 11
        SQ_LAG, VAR_LAG, QN_LAG = 1, 1, 2
        QT_LAG, QK_LAG, REST_LAG = 5, 6, 6
        PREP_FIRST, PREP_STEP = 4, 10
        SUMS_LAG, CENTRE_LAG, SCALE_LAG, W_HI_LAG, W_LO_LAG = 2, 2, 3, 4, 5
        TAIL = 4 + STORE_LAG
        STAGE_SLOTS = [SLOTS - UNITS + 2 + 3 * n for n in range(PROJ_PIECES)]
        CONVERT_LAG = 6

        def slots(last):
            return range(SLOTS + (TAIL if last else 0))

        def unit_at(slot, lag, first):
            u = slot - lag
            return [u] if u < SLOTS and (u >= 0 or not first) else []

        def head_at(slot, lag, first):
            u = slot - lag - (TT - 1)
            return [u // TT] if u % TT == 0 and u < SLOTS and (u >= 0 or not first) else []

        def tile_at(slot, lag, first, last):
            k, odd = divmod(slot - lag - 1, 2)
            n = GROUP_TILES - TILES if last else GROUP_TILES
            return [k] if not odd and k < n and (k >= 0 or not first) else []

        def prep_at(slot, lag, last):
            return [c for c in range(CH) if PREP_FIRST + PREP_STEP * c + lag == slot and not last]

        def tile_place(k):
            return (k // TILES + 1) % 2, k % TILES

        def stage_pieces(wp_d, wg_d, wu_d, wd_d):
            pieces = []
            wp_v = wp_d.rearrange("(f p) n -> p f n", p=P)
            for i in range(4):
                pieces.append((wp_v[:, 8 * i:8 * i + 8], wp[:, 8 * i:8 * i + 8], 0.0))
            for k, src in enumerate((wg_d, wu_d)):
                v = src.rearrange("(c p) n -> p c n", p=P)
                for i in range(2):
                    pieces.append((v[:, 2 * i:2 * i + 2], wgu[:, 2 * i:2 * i + 2, k * HID:(k + 1) * HID], -128.0))
            v = wd_d.rearrange("(c p) n -> p c n", p=P)
            pieces.append((v[:, 0:6], wd[:, 0:6], -128.0))
            pieces.append((v[:, 6:HC], wd[:, 6:HC], -128.0))
            return pieces

        block = stack.enter_context(nc.Block())

        @block.sync
        def _(sp):
            for first in (x_loaded, w_loaded, heads_stored, *out_stored):
                sp.sem_inc(first, 16 * FREE)
            sp.dma_start(col[:], cols).then_inc(cols_in, 16)
            def load_x(b):
                sp.wait_ge(x_loaded, 16 * (b + FREE))
                sp.wait_ge(ln_z, 2 * b - 3 + Z_FREE)
                x_dst = local[:, bass.ds((b % 2) * (2 * TT * DM), 2 * TT * DM)].bitcast(F32)
                sp.dma_start(x_dst.rearrange("p (t d) -> p t d", t=TT),
                             x_tiles[bass.ds(b, 1)].rearrange("o p t d -> (o p) t d")).then_inc(x_loaded, 16)

            def load_chunks(b):
                sp.wait_ge(w_loaded, 16 * (b + FREE))
                sp.wait_ge(w_ready, b - 1 + W_FREE)
                sp.dma_start(raw(b), wg_chunks[0, bass.ds(b, 1)].rearrange("o p n -> (o p) n")).then_inc(w_loaded, 16)
                sp.wait_ge(ctx_lo_done, b + FREE)
                sp.dma_start(ctx_raw[:], ctx_chunks[bass.ds(b, 1)].rearrange("o p t -> (o p) t")).then_inc(ctx_loaded, 16)

            load_x(0)
            with sp.Fori(0, B - 1) as b:
                load_x(b + 1)
                load_chunks(b)
            load_chunks(B - 1)

            def stage_load(n):
                src, dst, _ = pieces[n]
                if n >= 2:
                    sp.wait_ge(stage_done, n - 1)
                rows, width = src.shape[1], src.shape[2]
                view = stage[:, n % 2, 0:rows * width].bitcast(src.dtype)
                sp.dma_start(view.rearrange("p (r w) -> p r w", w=width), src).then_inc(stage_loaded[n % 2], 16)

            pieces = stage_pieces(w_proj, w_gate, w_up, w_down)
            def group(g, first, last):
                for slot in slots(last):
                    for c in prep_at(slot, -PREP_FIRST, last):
                        sp.wait_ge(w_loaded, 16 * (CH * g + CH + c + FREE))
                        sp.wait_ge(w_ready, CH * g + CH + c - 1 + W_FREE)
                        src = wg_chunks[bass.ds(g + 1, 1), c].rearrange("o p n -> (o p) n")
                        sp.dma_start(raw(c), src).then_inc(w_loaded, 16)
                    for H in head_at(slot, STORE_LAG, first):
                        if H % HEADS == HEADS - 1:
                            sp.wait_ge(heads_done, GROUP_HEADS * g + H + 1)
                            dst = heads_dram[H // HEADS % B, bass.ds(g + H // GROUP_HEADS, 1)]
                            sp.dma_start(dst.rearrange("o p n -> (o p) n"), heads.rearrange("p h t -> p (h t)"))\
                                .then_inc(heads_stored, 16)
                    if last and slot in STAGE_SLOTS:
                        if slot == STAGE_SLOTS[0]:
                            sp.wait_ge(proj_done, GROUP_TILES * G)
                        stage_load(STAGE_SLOTS.index(slot))

            group(0, True, False)
            with sp.Fori(1, G - 1) as g:
                group(g, False, False)

            group(G - 1, False, True)

            sp.wait_ge(heads_done, B * HEADS * G)
            sp.dma_start(sdown[:], s_down).then_inc(sdown_in, 16)
            sp.wait_ge(heads_stored, 16 * (B * G + FREE))
            sp.dma_start(heads_in.rearrange("p g h t -> p g (h t)"),
                         heads_dram[0].rearrange("g p n -> p g n")).then_inc(heads_back, 16)
            sp.dma_start(x_res[:], x_tiles[0]).then_inc(x_back, 16)
            for n in range(PROJ_PIECES, N_STAGE):
                stage_load(n)

            def store(b, tt):
                sp.wait_ge(out_ready, TT * b + tt + 1)
                dst = out_tiles[b, tt] if isinstance(b, int) else out_tiles[bass.ds(b, 1), tt].rearrange("o p d -> (o p) d")
                sp.dma_start(dst, y_out[:, tt % 2]).then_inc(out_stored[tt % 2], 16)

            with sp.Fori(1, B) as b:
                sp.wait_ge(pj_done, TT * b)
                sp.dma_start(heads_in.rearrange("p g h t -> p g (h t)"),
                             heads_dram[bass.ds(b, 1)].rearrange("o g p n -> p (o g) n")).then_inc(heads_back, 16)
                sp.wait_ge(x1_done, TT * b)
                sp.dma_start(x_res[:], x_tiles[bass.ds(b, 1)].rearrange("o p t d -> (o p) t d")).then_inc(x_back, 16)
                for tt in range(TT):
                    store(b - 1, tt)
            for tt in range(TT):
                store(B - 1, tt)
            for stored in out_stored:
                sp.wait_ge(stored, 16 * (B * TT // 2 + FREE))

        @block.tensor
        def _(pe):
            mm, tr = nc.tensor.matmul, nc.tensor.transpose
            pe.wait_ge(const_ready, 1)
            with pe.Fori(0, B) as b:
                pe.wait_ge(ln_z, 2 * b + 2 + Z_FREE)
                for c in range(CH):
                    if c >= 2:
                        pe.wait_ge(y4_done, CH * b + c - 1)
                    for tt in range(TT):
                        last = tr(ps_pt[c % 2][:, tt * P:(tt + 1) * P], z2[:, tt, c * P:(c + 1) * P], ident[:])
                    last.then_inc(zt_done, 1)

            def w_at(par, part, c, at, n):
                start = part * PART + c * GW + at
                return w_bf[:, bass.ds(par * PAR, PAR)][:, start:start + n]

            def project(b, i, half, par, t):
                c0 = i % TT
                tok = slice(b * T + c0 * P, b * T + (c0 + 1) * P)
                dst = ps_pj[i % 2]
                if half == 0 and not (isinstance(t, int) and t < 2):
                    pe.wait_ge(qn_done, t - 1)
                cross = i >= TT
                jobs = []
                if not cross:
                    jobs.append((0, 256, [(xq[:, 0, c, tok], c, part) for c in range(CH) for part in range(2)]))
                    jobs.append((256, 128, [(xq[:, 2, c, tok], c, part) for c in range(CH) for part in range(2)]))
                    jobs.append((384, 128, [(xq[:, 3, c, tok], c, part) for c in range(CH) for part in range(2)]))
                else:
                    jobs.append((0, 256, [(xq[:, 1, c, tok], c, part) for c in range(CH) for part in range(2)]))
                    jobs.append((256, 256, [(ctx_hi[:, c, tok], c, part) for c in range(CH) for part in range(2)] +
                                           [(ctx_lo[:, c, tok], c, 0) for c in range(CH)]))
                for at, n, terms in (jobs[:1] if half == 0 else jobs[1:]):
                    for k, (lhs, c, part) in enumerate(terms):
                        last = mm(dst[:, at:at + n], lhs, w_at(par, part, c, cross * 512 + at, n),
                                  start=(k == 0), stop=(k == len(terms) - 1))
                if half == 1:
                    last.then_inc(proj_done, 1)

            def turn_qk(i, t):
                pe.wait_ge(qn_done, t + 1)
                pe.wait_ge(full_done, t)
                for h in range(3):
                    last = tr(ps_qt[:, h * D:(h + 1) * D], qn[:, i % 2, h * D:(h + 1) * D], ident[:])
                last.then_inc(qt_done, 1)

            pe.wait_ge(w_ready, CH + W_FREE)
            pe.wait_ge(xq_done, B * CH)
            pe.wait_ge(ctx_lo_done, CH + FREE)
            for i in range(TILES):
                for half in range(2):
                    project(0, i, half, 0, i)
                if i >= 1:
                    turn_qk(i - 1, i - 1)
            turn_qk(TILES - 1, TILES - 1)

            def group(g, first, last):
                for slot in slots(last):
                    for u in unit_at(slot, PV_LAG + TT - 1, first):
                        H, tc = u // TT, u % TT
                        b, head = H // HEADS, H % HEADS
                        cross = head // HPG
                        if tc == 0:
                            pe.wait_ge(ptlo_done, SLOTS * g + TT * (H + 1))
                            pe.wait_ge(y_done, GROUP_HEADS * g + H + FREE)
                        vh, vl = v_hi[:, b % 2, cross, tc], v_lo[:, b % 2, cross, tc]
                        ph, pl = pt_hi[:, H % 2, tc], pt_lo[:, H % 2, tc]
                        mm(ps_o[:], vh, ph, start=(tc == 0), stop=False)
                        mm(ps_o[:], vh, pl, start=False, stop=False)
                        last_mm = mm(ps_o[:], vl, ph, start=False, stop=(tc == TT - 1))
                        if tc == TT - 1:
                            last_mm.then_inc(pv_done, 1)
                    for k in tile_at(slot, QT_LAG, first, last):
                        turn_qk(tile_place(k)[1], GROUP_TILES * g + TILES + k)
                    k, half = slot // 2, slot % 2
                    if k < (GROUP_TILES - TILES if last else GROUP_TILES):
                        b, i = k // TILES, k % TILES
                        if k == GROUP_TILES - TILES and half == 0:
                            pe.wait_ge(w_ready, CH * g + 2 * CH + W_FREE)
                        project((b + 1) % B, i, half, (g + 1) % 2 if b == B - 1 else g % 2, GROUP_TILES * g + TILES + k)
                    for u in unit_at(slot, 0, first):
                        b, head, qt = u // UNITS, u // TT % HEADS, u % TT
                        cross, hh = head // HPG, head % HPG
                        if u % (UNITS // 2) == 0:
                            pe.wait_ge(qklo_done, TILES * (B * g + b) + TT * (1 + cross))
                        if not first or u >= 2:
                            pe.wait_ge(exp_done, SLOTS * g + u - 1)
                        qs = slice(qt * P, (qt + 1) * P)
                        q_h, q_l = qk_hi[:, b % 2, cross, hh, qs], qk_lo[:, b % 2, cross, hh, qs]
                        k_h, k_l = qk_hi[:, b % 2, cross, 2], qk_lo[:, b % 2, cross, 2]
                        mm(ps_s[u % 2][:], q_h, k_h, start=True, stop=False)
                        mm(ps_s[u % 2][:], q_h, k_l, start=False, stop=False)
                        mm(ps_s[u % 2][:], q_l, k_h, start=False, stop=True).then_inc(s_done, 1)
                    for u in unit_at(slot, TURN_LAG, first):
                        pe.wait_ge(norm_done, SLOTS * g + u + 1)
                        if not first or u >= 2:
                            pe.wait_ge(ptlo_done, SLOTS * g + u - 1)
                        for tc in range(TT):
                            last_tr = tr(ps_pt[u % 2][:, tc * P:(tc + 1) * P], p_norm[:, u % 2, tc * P:(tc + 1) * P],
                                         ident[:])
                        last_tr.then_inc(pt_done, 1)

            group(0, True, False)
            with pe.Fori(1, G - 1) as g:
                group(g, False, False)
            group(G - 1, False, True)

            def out_projection(b):
                pe.wait_ge(heads_back, 16 * (b + 1))
                for tt in range(TT):
                    if tt >= 2:
                        pe.wait_ge(x1_done, TT * b + tt - 1)
                    for f in range(G * HEADS):
                        last = mm(ps_s[tt % 2][:], heads_in[:, f // HEADS, f % HEADS, tt * P:(tt + 1) * P], wp[:, f],
                                  start=(f == 0), stop=(f == G * HEADS - 1))
                    last.then_inc(pj_done, 1)

            def turn_z(b):
                pe.wait_ge(ln_z, 2 * B + b + 1 + Z_FREE)
                for tt in range(TT):
                    if tt >= 2:
                        pe.wait_ge(ztlo_done, TT * b + tt - 1)
                    for c in range(CH):
                        last = tr(ps_pt[tt % 2][:, c * P:(c + 1) * P], z3[:, tt, c * P:(c + 1) * P], ident[:])
                    last.then_inc(z3t_done, 1)

            def gate_up(b):
                pe.wait_ge(ztlo_done, TT * (b + 1))
                for m in range(HC):
                    for k, bank, signal in ((0, ps_pj[m % 2], gate_done), (1, ps_up[m % 2], up_done)):
                        if m >= 2:
                            pe.wait_ge(hid_done, HC * b + m - 1)
                        for c in range(CH):
                            w = wgu[:, c, k * HID + m * P:k * HID + (m + 1) * P]
                            mm(bank[:], w, zt_hi[:, c], start=(c == 0), stop=False)
                            last = mm(bank[:], w, zt_lo[:, c], start=False, stop=(c == CH - 1))
                        last.then_inc(signal, 1)

            def down(b, overlapped):
                pe.wait_ge(hlo_done, HC * (b + 1))
                for tt in range(TT):
                    if tt >= 2:
                        pe.wait_ge(scaled_done, TT * b + tt - 1)
                    elif overlapped:
                        pe.wait_ge(x1_done, TT * (b + 1) + tt + 3)
                    for m in range(HC):
                        ts = slice(tt * P, (tt + 1) * P)
                        mm(ps_s[tt % 2][:], h_hi[:, m, ts], wd[:, m], start=(m == 0), stop=False)
                        last = mm(ps_s[tt % 2][:], h_lo[:, m, ts], wd[:, m], start=False, stop=(m == HC - 1))
                    last.then_inc(down_done, 1)

            pe.wait_ge(stage_done, PROJ_PIECES)
            out_projection(0)
            turn_z(0)
            pe.wait_ge(stage_done, N_STAGE)
            gate_up(0)
            with pe.Fori(1, B) as b:
                out_projection(b)
                down(b - 1, True)
                turn_z(b)
                gate_up(b)
            down(B - 1, False)

        @block.scalar
        def _(act):
            a = nc.scalar.activation
            act.sem_inc(y_done, FREE)

            def weight_hi(par, c, count):
                act.wait_ge(w_scaled, count)
                act.sem_inc(waited_act, 1)
                a(w_bf[:, bass.ds(par * PAR + c * GW, GW)], raw(c), ACT.Copy).then_inc(w_hi_done, 1)

            act.wait_ge(scales_ready, 1)
            with act.Fori(0, B) as b:
                for c in range(CH):
                    act.wait_ge(zt_done, CH * b + c + 1)
                    if c >= 2:
                        act.wait_ge(xq_done, CH * b + c - 1)
                    for s in range(SETS):
                        k = s * CH + c
                        last = a(y4[:, c % 2, s * T:(s + 1) * T], ps_pt[c % 2][:], ACT.Identity,
                                 scale=ln_scale[:, k:k + 1], bias=ln_bias[:, k:k + 1])
                    last.then_inc(y4_done, 1)
                    if c == 1:
                        act.wait_ge(ctx_loaded, 16 * (b + 1))
                        act.sem_inc(waited_act, 1)
                        a(ctx_hi[:, bass.ds(b, 1)].rearrange("p o t -> p (o t)"), ctx_raw[:], ACT.Copy)\
                            .then_inc(ctx_hi_done, 1)
                    if c == 2:
                        weight_hi(0, b, b + 1)

            def squares(i, t):
                act.wait_ge(proj_done, t + 1)
                act.wait_ge(red_done, t)
                a(sq[:], ps_pj[i % 2][:, 0:3 * D], ACT.Square).then_inc(sq_done, 1)

            def v_part(b, i, t):
                a(v_hi[:, b % 2, i // TT, i % TT], ps_pj[i % 2][:, 3 * D:4 * D], ACT.Copy).then_inc(vhi_done, 1)

            def qk_part(b, i, t):
                act.wait_ge(qt_done, t + 1)
                act.wait_ge(qklo_done, t)
                cross, ts = i // TT, slice((i % TT) * P, (i % TT + 1) * P)
                w, bias = qscaled[:, 2 * cross:2 * cross + 1], qscaled[:, 2 * cross + 1:2 * cross + 2]
                kw, kb = ("kxln_w", "kxln_b") if cross else ("kln_w", "kln_b")
                q_in, k_in = ps_qt[:, 0:2 * D], ps_qt[:, 2 * D:3 * D]
                a(qk_hi[:, b % 2, cross, 0:2, ts], q_in.rearrange("p (h t) -> p h t", h=2), ACT.Identity, bias=bias, scale=w)
                a(qk_hi[:, b % 2, cross, 2, ts], k_in, ACT.Identity, bias=c_(kb), scale=c_(kw))
                a(qk_full[:, 0:2 * D], q_in, ACT.Identity, bias=bias, scale=w)
                a(qk_full[:, 2 * D:3 * D], k_in, ACT.Identity, bias=c_(kb), scale=c_(kw)).then_inc(full_done, 1)

            act.wait_ge(xq_done, B * CH)
            for i in range(TILES):
                squares(i, i)
                v_part(0, i, i)
                if i >= 1:
                    qk_part(0, i - 1, i - 1)
            qk_part(0, TILES - 1, TILES - 1)

            def convert(n):
                src, dst, offset = stage_pieces(w_proj, w_gate, w_up, w_down)[n]
                act.wait_ge(stage_loaded[n % 2], 16 * (n // 2 + 1))
                rows, width = src.shape[1], src.shape[2]
                raw = stage[:, n % 2, 0:rows * width].bitcast(src.dtype).rearrange("p (r w) -> p r w", w=width)
                a(dst, raw, ACT.Copy, bias=offset).then_inc(stage_done, 1)

            def group(g, first, last):
                for slot in slots(last):
                    for k in tile_at(slot, SQ_LAG, first, last):
                        b, i = tile_place(k)
                        t = GROUP_TILES * g + TILES + k
                        squares(i, t)
                        v_part(b, i, t)
                    for u in unit_at(slot, HI_LAG, first):
                        H, qt = u // TT, u % TT
                        act.wait_ge(pt_done, SLOTS * g + u + 1)
                        if qt == 0 and (not first or H >= 2):
                            act.wait_ge(pv_done, GROUP_HEADS * g + H - 1)
                        a(pt_hi[:, H % 2, :, qt * P:(qt + 1) * P], ps_pt[u % 2].rearrange("p (c t) -> p c t", c=TT),
                          ACT.Copy).then_inc(pthi_done, 1)
                    for k in tile_at(slot, QK_LAG, first, last):
                        qk_part(*tile_place(k), GROUP_TILES * g + TILES + k)
                    for H in head_at(slot, Y_LAG, first):
                        act.wait_ge(pv_done, GROUP_HEADS * g + H + 1)
                        if not first or H >= 2:
                            act.wait_ge(heads_done, GROUP_HEADS * g + H - 1)
                        act.sem_inc(waited_act, 1)
                        column = HEADS * (g + H // GROUP_HEADS) + H % HEADS
                        a(y[:, H % 2], ps_o[:], ACT.Copy, scale=rsmooth[:, bass.ds(column, 1)]).then_inc(y_done, 1)
                    for c in prep_at(slot, W_HI_LAG, last):
                        weight_hi((g + 1) % 2, c, CH * g + CH + c + 1)
                    for u in unit_at(slot, EXP_LAG, first):
                        act.wait_ge(max_done, SLOTS * g + u + 1)
                        if not first or u >= 2:
                            act.wait_ge(norm_done, SLOTS * g + u - 1)
                        a(p_exp[:, u % 2], ps_s[u % 2][:], ACT.Exp, bias=neg_max[:, u % 4:u % 4 + 1],
                          accum_out=p_sum[:, u % 4:u % 4 + 1]).then_inc(exp_done, 1)
                    if last and slot - CONVERT_LAG in STAGE_SLOTS:
                        convert(STAGE_SLOTS.index(slot - CONVERT_LAG))

            group(0, True, False)
            with act.Fori(1, G - 1) as g:
                group(g, False, False)
            group(G - 1, False, True)
            for n in range(PROJ_PIECES, N_STAGE):
                convert(n)

            def finish(b):
                for tt in range(TT):
                    act.wait_ge(z3t_done, TT * b + tt + 1)
                    a(zt_hi[:, :, tt * P:(tt + 1) * P], ps_pt[tt % 2].rearrange("p (c t) -> p c t", c=CH), ACT.Copy)\
                        .then_inc(zthi_done, 1)

                def h_part(m):
                    act.wait_ge(hid_done, HC * b + m + 1)
                    a(h_hi[:, m], hid[:, m % 2], ACT.Copy).then_inc(hhi_done, 1)

                for m in range(HC):
                    act.wait_ge(gate_done, HC * b + m + 1)
                    if m >= 2:
                        act.wait_ge(hid_done, HC * b + m - 1)
                    a(silu[:, m % 2], ps_pj[m % 2][:], ACT.Silu, scale=c_("s_gate", m)).then_inc(silu_done, 1)
                    if m >= 1:
                        h_part(m - 1)
                h_part(HC - 1)

            with act.Fori(0, B) as b:
                finish(b)

        @block.gpsimd
        def _(pool):
            nc.gpsimd.memset(ident[:], 0.0).then_inc(ident_zero, 1)
            pool.wait_ge(ident_zero, 1)
            nc.gpsimd.affine_select(out=ident[:], in_=ident[:], compare_op=ALU.not_equal, fill=1.0, base=0,
                                    pattern=[[-1, P]], channel_multiplier=1).then_inc(const_ready, 1)
            nc.gpsimd.memset(minus_half[:], -0.5).then_inc(const_ready, 1)
            tt_ = nc.gpsimd.tensor_tensor

            def spread_cols(v):
                return v.unsqueeze(2).to_broadcast([P, 8, D])

            def by_head(c):
                return raw(c).rearrange("p (k d) -> p k d", k=8)

            def weight_centre(c, count):
                pool.wait_ge(w_step, 2 * count)
                tt_(by_head(c), by_head(c), spread_cols(w_mean[:]), ALU.subtract).then_inc(w_centred, 1)

            def weight_scale(c, count):
                pool.wait_ge(w_centred, count)
                tt_(by_head(c), by_head(c), spread_cols(wscale[:, bass.ds(8 * c, 8)]), ALU.mult).then_inc(w_scaled, 1)

            def power(n):
                pool.wait_ge(ln_var, n + 1)
                tt_(rstd[:], spread[:], minus_half[:, 0:TT], ALU.pow).then_inc(ln_rstd, 1)

            pool.wait_ge(const_ready, 2)
            pool.wait_ge(scales_ready, 1)
            power(0)
            power(1)

            def prepare_weights(b):
                weight_centre(b, b + 1)
                weight_scale(b, b + 1)

            def rests(b):
                pool.wait_ge(w_hi_done, b + 1)
                tt_(w_bf[:, bass.ds(b * GW + PART, GW)], raw(b), w_bf[:, bass.ds(b * GW, GW)], ALU.subtract)\
                    .then_inc(w_ready, 1)
                pool.wait_ge(ctx_hi_done, b + 1)
                tt_(ctx_lo[:, bass.ds(b, 1)].rearrange("p o t -> p (o t)"), ctx_raw[:],
                    ctx_hi[:, bass.ds(b, 1)].rearrange("p o t -> p (o t)"), ALU.subtract).then_inc(ctx_lo_done, 1)

            with pool.Fori(0, B - 1) as b:
                power(2 * b + 2)
                prepare_weights(b)
                power(2 * b + 3)
                rests(b)
            prepare_weights(B - 1)
            rests(B - 1)

            def head_power(i, t):
                pool.wait_ge(var_done, t + 1)
                tt_(head_rstd[:, i % 2, 0:3], head_var[:, i % 2, 0:3], minus_half[:, 0:3], ALU.pow).then_inc(rstd_done, 1)

            def qk_rest(b, i, t):
                pool.wait_ge(full_done, t + 1)
                cross, ts = i // TT, slice((i % TT) * P, (i % TT + 1) * P)
                tt_(qk_lo[:, b % 2, cross, :, ts], qk_full[:].rearrange("p (h t) -> p h t", h=3),
                    qk_hi[:, b % 2, cross, :, ts], ALU.subtract).then_inc(qklo_done, 1)

            for i in range(TILES):
                head_power(i, i)
                if i >= 1:
                    qk_rest(0, i - 1, i - 1)
            qk_rest(0, TILES - 1, TILES - 1)

            def group(g, first, last):
                for slot in slots(last):
                    for c in prep_at(slot, CENTRE_LAG, last):
                        weight_centre(c, CH * g + CH + c + 1)
                    for c in prep_at(slot, SCALE_LAG, last):
                        weight_scale(c, CH * g + CH + c + 1)
                    for k in tile_at(slot, VAR_LAG, first, last):
                        head_power(tile_place(k)[1], GROUP_TILES * g + TILES + k)
                    for u in unit_at(slot, NORM_LAG, first):
                        pool.wait_ge(rsum_done, SLOTS * g + u + 1)
                        if not first or u >= 2:
                            pool.wait_ge(pt_done, SLOTS * g + u - 1)
                        tt_(p_norm[:, u % 2], p_exp[:, u % 2], r_sum[:, u % 4:u % 4 + 1].to_broadcast([P, T]), ALU.mult)\
                            .then_inc(norm_done, 1)
                    for k in tile_at(slot, REST_LAG, first, last):
                        qk_rest(*tile_place(k), GROUP_TILES * g + TILES + k)

            group(0, True, False)
            with pool.Fori(1, G - 1) as g:
                group(g, False, False)
            group(G - 1, False, True)

            with pool.Fori(0, B) as b:
                power(2 * B + b)
                for m in range(HC):
                    pool.wait_ge(hhi_done, HC * b + m + 1)
                    tt_(h_lo[:, m], hid[:, m % 2], h_hi[:, m], ALU.subtract).then_inc(hlo_done, 1)

        @block.vector
        def _(dve):
            v = nc.vector
            dve.sem_inc(w_ready, W_FREE)
            dve.sem_inc(ln_z, Z_FREE)
            dve.sem_inc(ctx_lo_done, FREE)
            v.memset(centre[:], 1.0 / D).then_inc(ones_set, 1)
            dve.wait_ge(ones_set, 1)
            dve.wait_ge(cols_in, 16)
            v.reciprocal(rscale, c_("in_scale", 0, SETS * CH)).then_inc(ones_set, 1)
            v.reciprocal(rsmooth[:], c_("smooth", 0, NH * 2))
            v.tensor_tensor(pscale[:], c_("proj_in"), c_("proj_w"), ALU.mult)
            for k, name in enumerate(("qln_w", "qln_b", "qxln_w", "qxln_b")):
                v.tensor_scalar(qscaled[:, k:k + 1], c_(name), float(D) ** -0.5, None, ALU.mult)
            v.memset(centre[:, 3:4], 0.0)
            v.memset(centre[:, 7:8], 0.0)
            v.memset(wscale[:], 1.0).then_inc(ones_set, 1)
            dve.wait_ge(ones_set, 3)
            for s in range(SETS):
                sets = slice(s * CH, (s + 1) * CH)
                v.tensor_tensor(ln_scale[:, sets], c_("ln_w", 0, CH), rscale[:, sets], ALU.mult)
                v.tensor_tensor(ln_bias[:, sets], c_("ln_b", 0, CH), rscale[:, sets], ALU.mult)
            for k, s in ((0, 0), (1, 0), (2, 2), (3, 3), (4, 1), (5, 1)):
                last = v.tensor_scalar(wscale[:].rearrange("p (c k) -> p c k", k=8)[:, :, k], c_("in_scale", s * CH, CH),
                                       c_("w_scale", s), None, ALU.mult)
            last.then_inc(scales_ready, 1)
            dve.wait_ge(scales_ready, 1)

            def weight_sums(c, count):
                dve.wait_ge(w_loaded, 16 * (count + FREE))
                v.tensor_reduce(w_sum[:], raw(c).rearrange("p (k d) -> p k d", k=8), AX_X, ALU.add).then_inc(w_step, 1)
                dve.wait_ge(w_step, 2 * count - 1)
                v.tensor_tensor(w_mean[:], w_sum[:], centre[:], ALU.mult).then_inc(w_step, 1)

            def weight_lo(par, c, count):
                dve.wait_ge(w_hi_done, count)
                hi = w_bf[:, bass.ds(par * PAR + c * GW, GW)]
                lo = w_bf[:, bass.ds(par * PAR + c * GW + PART, GW)]
                v.tensor_tensor(lo, raw(c), hi, ALU.subtract).then_inc(w_ready, 1)

            def ln_stats(src):
                for tt in range(TT):
                    v.bn_stats(stats[:, tt], src(tt)).then_inc(ln_step, 1)

            def ln_variance(n):
                dve.wait_ge(ln_step, LN_STEPS * n + TT)
                dve.sem_inc(waited_dve, 1)
                for tt in range(TT):
                    v.bn_aggr(moments[:, tt], stats[:, tt]).then_inc(ln_step, 1)
                dve.wait_ge(ln_step, LN_STEPS * (n + 1))
                v.tensor_scalar(spread[:], moments[:, :, 1], EPS, None, ALU.add).then_inc(ln_var, 1)

            def ln_apply(n, src, dst):
                dve.wait_ge(ln_rstd, n + 1)
                for tt in range(TT):
                    last = v.tensor_scalar(dst[:, tt], src(tt), moments[:, tt, 0:1], rstd[:, tt:tt + 1],
                                           ALU.subtract, ALU.mult)
                last.then_inc(ln_z, 1)

            def layer_norm(n, src, dst):
                ln_stats(src)
                ln_variance(n)
                ln_apply(n, src, dst)

            def quantise(n, dst, val, magnitude, total, signal, free=None):
                at = QUANT_STEPS * n
                v.tensor_scalar(val, val, FP8_MAX, -FP8_MAX, ALU.min, ALU.max).then_inc(quant_step, 1)
                dve.wait_ge(quant_step, at + 1)
                v.tensor_scalar(magnitude.bitcast(I16), val.bitcast(I16), EXPONENT, None, ALU.bitwise_and)\
                    .then_inc(quant_step, 1)
                dve.wait_ge(quant_step, at + 2)
                v.tensor_scalar(magnitude, magnitude, MIN_BINADE, KEEP4, ALU.max, ALU.mult).then_inc(quant_step, 1)
                dve.wait_ge(quant_step, at + 3)
                v.tensor_tensor(total, val, magnitude, ALU.add).then_inc(quant_step, 1)
                dve.wait_ge(quant_step, at + 4)
                if free:
                    free()
                shape = dst.shape
                if len(shape) == 3:
                    total = total.rearrange("p (s t) -> p s t", t=shape[2])
                    magnitude = magnitude.rearrange("p (s t) -> p s t", t=shape[2])
                v.tensor_tensor(dst, total, magnitude, ALU.subtract).then_inc(signal, 1)

            def x_at(b):
                xb = local[:, bass.ds((b % 2) * (2 * TT * DM), 2 * TT * DM)].bitcast(F32)
                return lambda tt: xb[:, tt * DM:(tt + 1) * DM]

            def z1_at(tt):
                return z1[:, tt]

            def quantise_chunk(b, c):
                dve.wait_ge(y4_done, CH * b + c + 1)
                quantise(CH * b + c, xq[:, :, c, bass.ds(b * T, T)], y4[:, c % 2], mag4, sum4, xq_done)

            dve.wait_ge(x_loaded, 16 * (1 + FREE))
            layer_norm(0, x_at(0), z1)
            dve.wait_ge(ln_z, 1 + Z_FREE)
            layer_norm(1, z1_at, z2)
            with dve.Fori(0, B - 1) as b:
                weight_sums(b, b + 1)
                n = 2 * b + 2
                dve.wait_ge(x_loaded, 16 * (b + 2 + FREE))
                dve.sem_inc(waited_dve, 1)
                ln_stats(x_at(b + 1))
                quantise_chunk(b, 0)
                ln_variance(n)
                quantise_chunk(b, 1)
                ln_apply(n, x_at(b + 1), z1)
                dve.wait_ge(ln_z, n + 1 + Z_FREE)
                dve.sem_inc(waited_dve, 1)
                ln_stats(z1_at)
                quantise_chunk(b, 2)
                ln_variance(n + 1)
                quantise_chunk(b, 3)
                dve.wait_ge(zt_done, CH * (b + 1))
                ln_apply(n + 1, z1_at, z2)
            weight_sums(B - 1, B)
            for c in range(CH):
                quantise_chunk(B - 1, c)

            def head_variance(i, t):
                dve.wait_ge(sq_done, t + 1)
                v.tensor_reduce(sq_sum[:, i % 2, 0:3], sq[:].rearrange("p (h d) -> p h d", h=3), AX_X, ALU.add)\
                    .then_inc(red_done, 1)
                dve.wait_ge(red_done, t + 1)
                v.tensor_scalar(head_var[:, i % 2, 0:3], sq_sum[:, i % 2, 0:3], 1.0 / D, EPS, ALU.mult, ALU.add)\
                    .then_inc(var_done, 1)

            def v_rest(b, i, t):
                dve.wait_ge(vhi_done, t + 1)
                v.tensor_tensor(v_lo[:, b % 2, i // TT, i % TT], ps_pj[i % 2][:, 3 * D:4 * D],
                                v_hi[:, b % 2, i // TT, i % TT], ALU.subtract).then_inc(vlo_done, 1)

            def head_norm(i, t):
                dve.wait_ge(rstd_done, t + 1)
                if not isinstance(t, int) or t >= 2:
                    dve.wait_ge(qt_done, t - 1)
                v.tensor_tensor(qn[:, i % 2].rearrange("p (h d) -> p h d", h=3),
                                ps_pj[i % 2][:, 0:3 * D].rearrange("p (h d) -> p h d", h=3),
                                head_rstd[:, i % 2, 0:3].unsqueeze(2).to_broadcast([P, 3, D]), ALU.mult)\
                    .then_inc(qn_done, 1)

            for i in range(TILES):
                head_variance(i, i)
                v_rest(0, i, i)
                head_norm(i, i)

            def group(g, first, last):
                for slot in slots(last):
                    for c in prep_at(slot, SUMS_LAG, last):
                        weight_sums(c, CH * g + CH + c + 1)
                    for u in unit_at(slot, MAX_LAG, first):
                        dve.wait_ge(s_done, SLOTS * g + u + 1)
                        v.tensor_reduce(neg_max[:, u % 4:u % 4 + 1], ps_s[u % 2][:], AX_X, ALU.max, negate=True)\
                            .then_inc(max_done, 1)
                    for H in head_at(slot, QUANT_LAG, first):
                        head = H % HEADS
                        dve.wait_ge(y_done, GROUP_HEADS * g + H + 1 + FREE)

                        def stored():
                            if head == 0:
                                dve.wait_ge(heads_stored, 16 * (B * g + H // HEADS + FREE))
                        quantise(B * CH + GROUP_HEADS * g + H, heads[:, head], y[:, H % 2], mag, summed, heads_done, stored)
                    for u in unit_at(slot, SUM_LAG, first):
                        dve.wait_ge(exp_done, SLOTS * g + u + 1)
                        v.reciprocal(r_sum[:, u % 4:u % 4 + 1], p_sum[:, u % 4:u % 4 + 1]).then_inc(rsum_done, 1)
                    for c in prep_at(slot, W_LO_LAG, last):
                        weight_lo((g + 1) % 2, c, CH * g + CH + c + 1)
                    for k in tile_at(slot, QN_LAG, first, last):
                        head_norm(tile_place(k)[1], GROUP_TILES * g + TILES + k)
                    for k in tile_at(slot, VAR_LAG, first, last):
                        head_variance(tile_place(k)[1], GROUP_TILES * g + TILES + k)
                    for u in unit_at(slot, LO_LAG, first):
                        H, qt = u // TT, u % TT
                        dve.wait_ge(pthi_done, SLOTS * g + u + 1)
                        dst = slice(qt * P, (qt + 1) * P)
                        v.tensor_tensor(pt_lo[:, H % 2, :, dst], ps_pt[u % 2].rearrange("p (c t) -> p c t", c=TT),
                                        pt_hi[:, H % 2, :, dst], ALU.subtract).then_inc(ptlo_done, 1)
                    for k in tile_at(slot, VAR_LAG, first, last):
                        v_rest(*tile_place(k), GROUP_TILES * g + TILES + k)

            group(0, True, False)
            with dve.Fori(1, G - 1) as g:
                group(g, False, False)
            group(G - 1, False, True)

            def x1_at(b, tt):
                if isinstance(b, int):
                    at = (b % 2) * TT * DM + tt * DM
                    return x1[:, at:at + DM]
                return x1[:, bass.ds((b % 2) * (TT * DM) + tt * DM, DM)]

            def residual(b):
                dve.wait_ge(x_back, 16 * (b + 1))
                for tt in range(TT):
                    dve.wait_ge(pj_done, TT * b + tt + 1)
                    v.scalar_tensor_tensor(x1_at(b, tt), ps_s[tt % 2][:], pscale[:, 0:1], x_res[:, tt], ALU.mult, ALU.add)\
                        .then_inc(x1_done, 1)
                dve.wait_ge(x1_done, TT * (b + 1))
                dve.sem_inc(waited_dve, 1)
                layer_norm(2 * B + b, lambda tt: x1_at(b, tt), z3)

            def output(b):
                for tt in range(TT):
                    dve.wait_ge(down_done, TT * b + tt + 1)
                    v.tensor_tensor(scaled[:, tt % 2], ps_s[tt % 2][:], sdown[:], ALU.mult).then_inc(scaled_done, 1)
                    dve.wait_ge(scaled_done, TT * b + tt + 1)
                    dve.wait_ge(out_stored[tt % 2], 16 * (TT // 2 * b + tt // 2 + FREE))
                    v.tensor_tensor(y_out[:, tt % 2], scaled[:, tt % 2], x1_at(b, tt), ALU.add).then_inc(out_ready, 1)

            def hidden(b):
                for tt in range(TT):
                    dve.wait_ge(zthi_done, TT * b + tt + 1)
                    dst = slice(tt * P, (tt + 1) * P)
                    v.tensor_tensor(zt_lo[:, :, dst], ps_pt[tt % 2].rearrange("p (c t) -> p c t", c=CH), zt_hi[:, :, dst],
                                    ALU.subtract).then_inc(ztlo_done, 1)
                for m in range(HC):
                    dve.wait_ge(silu_done, HC * b + m + 1)
                    dve.wait_ge(up_done, HC * b + m + 1)
                    if m >= 2:
                        dve.wait_ge(hlo_done, HC * b + m - 1)
                    v.scalar_tensor_tensor(hid[:, m % 2], ps_up[m % 2][:], c_("s_up", m), silu[:, m % 2],
                                           ALU.mult, ALU.mult).then_inc(hid_done, 1)

            dve.wait_ge(sdown_in, 16)
            residual(0)
            hidden(0)
            with dve.Fori(1, B) as b:
                residual(b)
                output(b - 1)
                hidden(b)
            output(B - 1)


def kernel(**inputs):
    import concourse.bacc as bacc
    from concourse.bass_utils import run_bass_kernel_spmd

    a = {k: np.asarray(v) for k, v in inputs.items()}
    xa = {k[len("L0_xattn_"):]: v for k, v in a.items() if k.startswith("L0_xattn_")}
    ff = {k[len("L0_ffn_"):]: v for k, v in a.items() if k.startswith("L0_ffn_")}

    def per_group(w, n):
        return w.reshape(G, n, DM).transpose(0, 2, 1)

    kvx = xa["w_kv_x"]
    w_group = np.concatenate([per_group(xa["wq"], 256), per_group(xa["wk"], 128), per_group(xa["wv"], 128),
                              per_group(xa["wqx"], 256), per_group(kvx[:G * D], 128), per_group(kvx[G * D:], 128)], axis=2)
    order = [f for g in range(G) for f in (2 * g, 2 * g + 1, NH + 2 * g, NH + 2 * g + 1)]
    w_proj = xa["wproj"].T.reshape(2 * NH, D, DM)[order].reshape(2 * NH * D, DM)
    smooth = xa["proj_smooth"].reshape(2 * NH, D)[order]

    def column(v):
        return np.broadcast_to(v.reshape(1, 1), (P, 1))

    def chunked(v):
        return v.reshape(-1, P).T

    parts = {
        "ln_w": chunked(xa["ln_w"]), "ln_b": chunked(xa["ln_b"]),
        "in_scale": np.concatenate([chunked(xa[f"{n}_in_scale"]) for n in ("q", "qx", "k", "v")], axis=1),
        "w_scale": np.concatenate([column(xa[f"w{n}_scale"]) for n in ("q", "qx", "k", "v")], axis=1),
        **{n: chunked(xa[n]) for n in ("qln_w", "qln_b", "qxln_w", "qxln_b", "kln_w", "kln_b", "kxln_w", "kxln_b")},
        "smooth": smooth.T, "s_gate": chunked(ff["s_gate"]), "s_up": chunked(ff["s_up"]),
        "proj_in": column(xa["proj_in_scale"]), "proj_w": column(xa["proj_w_scale"]),
    }
    arrays = {
        "x": a["x"].reshape(NTOK, DM),
        "ctx_t": a["ctx_2048"].reshape(NTOK, DM).T,
        "w_group": w_group,
        "w_proj": w_proj,
        "w_gate": ff["wq_gate"].T,
        "w_up": ff["wq_up"].T,
        "w_down": ff["wq_down"].T,
        "cols": np.concatenate([parts[n] for n in COLS], axis=1),
        "s_down": np.broadcast_to(ff["s_down"].reshape(1, DM), (P, DM)),
    }
    arrays = {k: np.ascontiguousarray(v) for k, v in arrays.items()}

    nc = bacc.Bacc("TRN2", target_bir_lowering=False, num_devices=1)
    args = [nc.dram_tensor(n, v.shape, mybir.dt.from_np(v.dtype), kind="ExternalInput").ap() for n, v in arrays.items()]
    out = nc.dram_tensor("out", (NTOK, DM), F32, kind="ExternalOutput").ap()
    block_kernel(nc, *args, out)
    r = run_bass_kernel_spmd(nc, [arrays], core_ids=[0])
    return r.results[0]["out"].reshape(B, T, DM)
```

```python
from contextlib import ExitStack

import numpy as np

import concourse.bass as bass
from concourse import mybir

F32 = mybir.dt.float32
BF16 = mybir.dt.bfloat16
I16 = mybir.dt.int16
I32 = mybir.dt.int32
ALU = mybir.AluOpType
ACT = mybir.ActivationFunctionType
AX_X = mybir.AxisListType.X

P = 128
B, T, DM = 4, 512, 512
NTOK = B * T
G, D = 8, 128
HPG = 2
NH = G * HPG
CH = DM // P
TT = T // P
HID = 1408
HC = HID // P
SETS = 4
GW = 8 * D
STAGE_SIZE = 4 * DM
HEADS = 2 * HPG
UNITS = HEADS * TT
TILES = 2 * TT
EPS = 1e-5
FP8_MAX = 448.0
EXPONENT = 0x7F80
MIN_BINADE = 2.0 ** -6
KEEP4 = 24.0

FREE = 1
W_FREE = 2
Y_FREE = 2
QUANT_STEPS = 4
QUANT_FREE = 2 * QUANT_STEPS
Z_FREE = 2 * 2

COLS = {}
for _name, _n in (("ln_w", CH), ("ln_b", CH), ("in_scale", SETS * CH), ("w_scale", SETS), ("qln_w", 1), ("qln_b", 1),
                  ("qxln_w", 1), ("qxln_b", 1), ("kln_w", 1), ("kln_b", 1), ("kxln_w", 1), ("kxln_b", 1),
                  ("smooth", NH * 2), ("s_gate", HC), ("s_up", HC), ("proj_in", 1), ("proj_w", 1)):
    COLS[_name] = (sum(n for _, n in COLS.values()), _n)
NCOLS = sum(n for _, n in COLS.values())


def block_kernel(nc, x, ctx_t, w_group, w_proj, w_gate, w_up, w_down, cols, s_down, out):
    x_tiles = x.rearrange("(b t p) d -> b p t d", b=B, p=P)
    out_tiles = out.rearrange("(b t p) d -> b t p d", b=B, p=P)
    ctx_chunks = ctx_t.rearrange("(c p) t -> c p t", p=P)
    wg_chunks = w_group.rearrange("g (c p) n -> g c p n", p=P)
    heads_dram = nc.dram_tensor("quantised_heads", (B, G, P, HEADS * T), BF16, kind="Internal").ap()

    stack = ExitStack()
    with stack:
        def sb(name, shape, dt):
            return stack.enter_context(nc.sbuf_tensor(name, shape, dt))

        def psum(name):
            return stack.enter_context(nc.psum_tensor(name, [P, 512], F32))

        def sem(name):
            return stack.enter_context(nc.semaphore(name))

        wide = sb("wide", [P, 65536], BF16)
        local = sb("local", [P, 35840], BF16)
        ln_scale = sb("ln_scale", [P, SETS * CH], F32)
        ln_bias = sb("ln_bias", [P, SETS * CH], F32)
        w_raw = sb("w_raw", [P, 2 * GW], F32)
        ident = sb("ident", [P, P], F32)
        col = sb("col", [P, NCOLS], F32)
        wscale = sb("wscale", [P, CH * 8], F32)
        rsmooth = sb("rsmooth", [P, NH * 2], F32)
        qscaled = sb("qscaled", [P, 4], F32)
        pscale = sb("pscale", [P, 1], F32)
        centre = sb("centre", [P, 8], F32)
        minus_half = sb("minus_half", [P, TT], F32)
        stats = sb("stats", [P, TT, 6], F32)
        moments = sb("moments", [P, TT, 2], F32)
        spread = sb("spread", [P, TT], F32)
        rstd = sb("rstd", [P, TT], F32)
        w_sum = sb("w_sum", [P, 8], F32)
        w_mean = sb("w_mean", [P, 8], F32)
        neg_max = sb("neg_max", [P, 4], F32)
        p_sum = sb("p_sum", [P, 4], F32)
        r_sum = sb("r_sum", [P, 4], F32)
        sq_sum = sb("sq_sum", [P, 2, 4], F32)
        head_var = sb("head_var", [P, 2, 4], F32)
        head_rstd = sb("head_rstd", [P, 2, 4], F32)

        class Carve:
            def __init__(self, region):
                self.region, self.at = region, 0

            def __call__(self, shape, dt):
                n = int(np.prod(shape)) * (2 if dt in (F32, I32) else 1)
                v = self.region[:, self.at:self.at + n]
                self.at += n
                if dt != BF16:
                    v = v.bitcast(dt)
                if len(shape) == 1:
                    return v
                names = "abcde"[:len(shape)]
                return v.rearrange(f"p ({' '.join(names)}) -> p {' '.join(names)}",
                                   **{k: s for k, s in zip(names[1:], shape[1:])})

        def c_(name, i=0, n=1):
            at = COLS[name][0] + i
            return col[:, at:at + n]

        carve = Carve(wide)
        xq = carve([SETS, CH, NTOK], BF16)
        ctx_hi = carve([CH, NTOK], BF16)
        ctx_lo = carve([CH, NTOK], BF16)
        PART, PAR = CH * GW, 2 * CH * GW
        w_bf = carve([2 * PAR], BF16)
        carve = Carve(wide)
        heads_in = carve([G, HEADS, T], BF16)
        wgu = carve([CH, 2 * HID], BF16)
        wd = carve([HC, DM], BF16)
        x_res = carve([TT, DM], F32)
        carve.at = 2 * CH * NTOK + SETS * CH * NTOK + PAR - G * HEADS * DM
        wp = carve([G * HEADS, DM], BF16)
        stage = carve([2, STAGE_SIZE], F32)
        carve = Carve(stage.rearrange("p a b -> p (a b)").bitcast(BF16))
        silu = carve([2, T], F32)
        hid = carve([2, T], F32)
        scaled = carve([2, DM], F32)
        carve = Carve(local)
        x_in = carve([2, TT, DM], F32)
        z1 = carve([TT, DM], F32)
        z2 = carve([TT, DM], F32)
        y4 = carve([2, SETS * T], BF16)
        mag4 = carve([2, SETS * T], BF16)
        sum4 = carve([2, SETS * T], BF16)
        ctx_raw = carve([NTOK], F32)
        rscale = mag4[:, 0, 0:2 * SETS * CH].bitcast(F32)
        carve = Carve(local)
        qk_hi = carve([2, 2, 3, T], BF16)
        qk_lo = carve([2, 2, 3, T], BF16)
        v_hi = carve([2, 2, TT, D], BF16)
        v_lo = carve([2, 2, TT, D], BF16)
        pt_hi = carve([2, TT, T], BF16)
        pt_lo = carve([2, TT, T], BF16)
        heads = carve([HEADS, T], BF16)
        y = carve([2, T], BF16)
        mag = carve([T], BF16)
        summed = carve([T], BF16)
        p_exp = carve([2, T], F32)
        p_norm = carve([2, T], F32)
        sq = carve([3 * D], F32)
        qn = carve([2, 3 * D], F32)
        qk_full = carve([3 * D], F32)
        start_full = [qk_full, p_norm[:, 0, 0:3 * D]]
        carve = Carve(local)
        x1 = carve([2 * TT * DM], F32)
        z3 = carve([TT, DM], F32)
        y_out = carve([2, DM], F32)
        sdown = carve([DM], F32)
        h_hi = carve([HC, T], BF16)
        h_lo = carve([HC, T], BF16)
        zt_hi = carve([CH, T], BF16)
        zt_lo = carve([CH, T], BF16)

        ps_s = [psum(f"ps_s{i}") for i in range(2)]
        ps_pt = [psum(f"ps_pt{i}") for i in range(2)]
        ps_pj = [psum(f"ps_pj{i}") for i in range(2)]
        ps_qt = psum("ps_qt")
        ps_o = psum("ps_o")
        ps_up = [ps_qt, ps_o]
        EARLY_BANKS = [*ps_pj, ps_qt]
        START_BANKS = [*ps_pj, *ps_s]

        def raw(c):
            return w_raw[:, bass.ds((c % 2) * GW, GW)]

        waited_act = sem("waited_act")
        waited_dve = sem("waited_dve")
        cols_in = sem("cols_in")
        ident_zero = sem("ident_zero")
        ones_set = sem("ones_set")
        const_ready = sem("const_ready")
        scales_ready = sem("scales_ready")
        x_loaded = sem("x_loaded")
        ctx_loaded = sem("ctx_loaded")
        ctx_hi_done = sem("ctx_hi_done")
        ctx_lo_done = sem("ctx_lo_done")
        ln_step = sem("ln_step")
        ln_var = sem("ln_var")
        ln_rstd = sem("ln_rstd")
        ln_z = sem("ln_z")
        zt_done = sem("zt_done")
        y4_done = sem("y4_done")
        quant_step = sem("quant_step")
        xq_even = sem("xq_even")
        xq_odd = sem("xq_odd")
        w_loaded = sem("w_loaded")
        w_step = sem("w_step")
        w_centred = sem("w_centred")
        w_scaled = sem("w_scaled")
        w_hi_done = sem("w_hi_done")
        w_ready = sem("w_ready")
        proj_done = sem("proj_done")
        sq_done = sem("sq_done")
        vhi_done = sem("vhi_done")
        vlo_done = sem("vlo_done")
        red_done = sem("red_done")
        var_done = sem("var_done")
        rstd_done = sem("rstd_done")
        qn_done = sem("qn_done")
        qt_done = sem("qt_done")
        full_done = sem("full_done")
        qklo_done = sem("qklo_done")
        s_done = sem("s_done")
        max_done = sem("max_done")
        exp_done = sem("exp_done")
        rsum_done = sem("rsum_done")
        norm_done = sem("norm_done")
        pt_done = sem("pt_done")
        pthi_done = sem("pthi_done")
        ptlo_done = sem("ptlo_done")
        pv_done = sem("pv_done")
        y_done = sem("y_done")
        heads_done = sem("heads_done")
        heads_stored = sem("heads_stored")
        stage_loaded = [sem(f"stage_loaded{i}") for i in range(2)]
        stage_done = sem("stage_done")
        early_done = sem("early_done")
        sdown_in = sem("sdown_in")
        heads_back = sem("heads_back")
        x_back = sem("x_back")
        pj_done = sem("pj_done")
        x1_done = sem("x1_done")
        z3t_done = sem("z3t_done")
        zthi_done = sem("zthi_done")
        ztlo_done = sem("ztlo_done")
        gate_done = sem("gate_done")
        up_done = sem("up_done")
        silu_done = sem("silu_done")
        hid_done = sem("hid_done")
        hhi_done = sem("hhi_done")
        hlo_done = sem("hlo_done")
        down_done = sem("down_done")
        scaled_done = sem("scaled_done")
        out_ready = sem("out_ready")
        out_stored = [sem(f"out_stored{i}") for i in range(2)]

        LN_STEPS = 2 * TT
        EARLY_ROW = G * HEADS - PAR // DM
        EARLY_PIECES = (G * HEADS - EARLY_ROW) // (GW // DM)
        ROWS = STAGE_SIZE // DM
        PROJ_PIECES = EARLY_ROW // ROWS
        N_STAGE = PROJ_PIECES + 2 * CH + -(-HC // ROWS)

        SLOTS = B * UNITS
        GROUP_TILES = B * TILES
        GROUP_HEADS = B * HEADS
        MAX_LAG, EXP_LAG, SUM_LAG, NORM_LAG = 1, 1, 2, 2
        TURN_LAG, HI_LAG, LO_LAG = 3, 4, 4
        PV_LAG, Y_LAG, QUANT_LAG, STORE_LAG = 6, 9, 10, 11
        SQ_LAG, VAR_LAG, QN_LAG = 1, 1, 2
        QT_LAG, QK_LAG, REST_LAG = 5, 6, 6
        PREP_FIRST, PREP_STEP = 4, 10
        SUMS_LAG, CENTRE_LAG, SCALE_LAG, W_HI_LAG, W_LO_LAG = 2, 2, 3, 4, 5
        TAIL = 4 + STORE_LAG
        EARLY_SLOTS = [2 + 5 * n for n in range(EARLY_PIECES)]
        CONVERT_LAG = 3
        STAGE_SLOTS = [SLOTS - UNITS + 2 + 2 * n for n in range(PROJ_PIECES)]
        STAGE_SLOTS += [SLOTS + CONVERT_LAG + n for n in range(TAIL - CONVERT_LAG - 3)]
        CONVERT_SLOTS = [slot + CONVERT_LAG for slot in STAGE_SLOTS]
        HEADS_SLOT = STORE_LAG + SLOTS - UNITS
        EARLY_TILES, EARLY_FIRST = 3, SLOTS + 3
        EARLY_STEP = -(-EARLY_TILES * G * HEADS // (SLOTS + TAIL - EARLY_FIRST))

        def slots(last):
            return range(SLOTS + (TAIL if last else 0))

        def unit_at(slot, lag, first):
            u = slot - lag
            return [u] if u < SLOTS and (u >= 0 or not first) else []

        def head_at(slot, lag, first):
            u = slot - lag - (TT - 1)
            return [u // TT] if u % TT == 0 and u < SLOTS and (u >= 0 or not first) else []

        def tile_at(slot, lag, first, last):
            k, odd = divmod(slot - lag - 1, 2)
            n = GROUP_TILES - TILES if last else GROUP_TILES
            return [k] if not odd and k < n and (k >= 0 or not first) else []

        def prep_at(slot, lag, last):
            return [c for c in range(CH) if PREP_FIRST + PREP_STEP * c + lag == slot and not last]

        def tile_place(k):
            return (k // TILES + 1) % 2, k % TILES

        START_LAG = 2

        def at_start(t):
            return isinstance(t, int) and t < TILES

        def full_of(i, t):
            return start_full[i % 2] if at_start(t) else qk_full

        def tile_bank(i, t):
            return START_BANKS[i % len(START_BANKS)] if at_start(t) else ps_pj[i % 2]

        def stage_pieces(wp_d, wg_d, wu_d, wd_d):
            pieces = []
            v = wp_d.rearrange("(f p) n -> p f n", p=P)
            for r in range(0, EARLY_ROW, ROWS):
                pieces.append((v[:, r:r + ROWS], wp[:, r:r + ROWS], 0.0))
            for k, src in enumerate((wg_d, wu_d)):
                v = src.rearrange("(c p) n -> p c n", p=P)
                for c in range(CH):
                    pieces.append((v[:, c:c + 1], wgu[:, c:c + 1, k * HID:(k + 1) * HID], -128.0))
            v = wd_d.rearrange("(c p) n -> p c n", p=P)
            for r in range(0, HC, ROWS):
                rows = slice(r, min(r + ROWS, HC))
                pieces.append((v[:, rows], wd[:, rows], -128.0))
            return pieces

        def early_piece(n):
            r = EARLY_ROW + n * (GW // DM)
            rows = slice(r, r + GW // DM)
            return w_proj.rearrange("(f p) n -> p f n", p=P)[:, rows], wp[:, rows]

        block = stack.enter_context(nc.Block())

        @block.sync
        def _(sp):
            for first in (x_loaded, w_loaded, heads_stored, *out_stored):
                sp.sem_inc(first, 16 * FREE)
            sp.dma_start(col[:], cols).then_inc(cols_in, 16)

            def load_x(b):
                sp.wait_ge(x_loaded, 16 * (b + FREE))
                sp.wait_ge(ln_z, 2 * b - 3 + Z_FREE)
                x_dst = local[:, bass.ds((b % 2) * (2 * TT * DM), 2 * TT * DM)].bitcast(F32)
                sp.dma_start(x_dst.rearrange("p (t d) -> p t d", t=TT),
                             x_tiles[bass.ds(b, 1)].rearrange("o p t d -> (o p) t d")).then_inc(x_loaded, 16)

            def load_weights(c):
                sp.wait_ge(w_loaded, 16 * (c + FREE))
                sp.wait_ge(w_ready, c - 1 + W_FREE)
                sp.dma_start(raw(c), wg_chunks[0, bass.ds(c, 1)].rearrange("o p n -> (o p) n")).then_inc(w_loaded, 16)

            def load_ctx(c):
                sp.wait_ge(ctx_lo_done, c + FREE)
                sp.dma_start(ctx_raw[:], ctx_chunks[bass.ds(c, 1)].rearrange("o p t -> (o p) t")).then_inc(ctx_loaded, 16)

            load_x(0)
            load_weights(0)
            with sp.Fori(0, B - 1) as b:
                load_x(b + 1)
                load_weights(b + 1)
                load_ctx(b)
            load_ctx(B - 1)

            def stage_load(n):
                src, dst, _ = pieces[n]
                if n >= 2:
                    sp.wait_ge(stage_done, n - 1)
                rows, width = src.shape[1], src.shape[2]
                view = stage[:, n % 2, 0:rows * width].bitcast(src.dtype)
                sp.dma_start(view.rearrange("p (r w) -> p r w", w=width), src).then_inc(stage_loaded[n % 2], 16)

            pieces = stage_pieces(w_proj, w_gate, w_up, w_down)

            def group(g, first, last):
                for slot in slots(last):
                    for c in prep_at(slot, -PREP_FIRST, last):
                        sp.wait_ge(w_loaded, 16 * (CH * g + CH + c + FREE))
                        sp.wait_ge(w_ready, CH * g + CH + c - 1 + W_FREE)
                        src = wg_chunks[bass.ds(g + 1, 1), c].rearrange("o p n -> (o p) n")
                        sp.dma_start(raw(c), src).then_inc(w_loaded, 16)
                    for H in head_at(slot, STORE_LAG, first):
                        if H % HEADS == HEADS - 1:
                            sp.wait_ge(heads_done, GROUP_HEADS * g + H + 1)
                            dst = heads_dram[H // HEADS % B, bass.ds(g + H // GROUP_HEADS, 1)]
                            sp.dma_start(dst.rearrange("o p n -> (o p) n"), heads.rearrange("p h t -> p (h t)"))\
                                .then_inc(heads_stored, 16)
                    if last and slot in EARLY_SLOTS:
                        n = EARLY_SLOTS.index(slot)
                        if n == 0:
                            sp.wait_ge(w_ready, CH * G + W_FREE)
                        sp.wait_ge(w_loaded, 16 * (CH * G + n + FREE))
                        if n >= 2:
                            sp.wait_ge(early_done, n - 1)
                        src, dst = early_piece(n)
                        sp.dma_start(raw(n).rearrange("p (r w) -> p r w", w=DM), src).then_inc(w_loaded, 16)
                    if last and slot in STAGE_SLOTS:
                        if slot == STAGE_SLOTS[0]:
                            sp.wait_ge(proj_done, GROUP_TILES * G)
                        stage_load(STAGE_SLOTS.index(slot))
                    if last and slot == HEADS_SLOT:
                        sp.wait_ge(heads_stored, 16 * (B * (G - 1) + 1 + FREE))
                        sp.dma_start(heads_in.rearrange("p g h t -> p g (h t)"),
                                     heads_dram[0].rearrange("g p n -> p g n")).then_inc(heads_back, 16)
                        sp.dma_start(x_res[:], x_tiles[0]).then_inc(x_back, 16)

            group(0, True, False)
            with sp.Fori(1, G - 1) as g:
                group(g, False, False)

            group(G - 1, False, True)

            for n in range(len(STAGE_SLOTS), N_STAGE):
                stage_load(n)
            sp.wait_ge(heads_done, B * HEADS * G)
            sp.dma_start(sdown[:], s_down).then_inc(sdown_in, 16)

            def store(b, tt):
                sp.wait_ge(out_ready, TT * b + tt + 1)
                dst = out_tiles[b, tt] if isinstance(b, int) else out_tiles[bass.ds(b, 1), tt].rearrange("o p d -> (o p) d")
                sp.dma_start(dst, y_out[:, tt % 2]).then_inc(out_stored[tt % 2], 16)

            sp.wait_ge(heads_stored, 16 * (B * G + FREE))
            with sp.Fori(1, B) as b:
                sp.wait_ge(pj_done, TT * b)
                sp.dma_start(heads_in.rearrange("p g h t -> p g (h t)"),
                             heads_dram[bass.ds(b, 1)].rearrange("o g p n -> p (o g) n")).then_inc(heads_back, 16)
                sp.wait_ge(x1_done, TT * b)
                sp.dma_start(x_res[:], x_tiles[bass.ds(b, 1)].rearrange("o p t d -> (o p) t d")).then_inc(x_back, 16)
                for tt in range(TT):
                    store(b - 1, tt)
            for tt in range(TT):
                store(B - 1, tt)
            for stored in out_stored:
                sp.wait_ge(stored, 16 * (B * TT // 2 + FREE))

        @block.tensor
        def _(pe):
            mm, tr = nc.tensor.matmul, nc.tensor.transpose
            pe.wait_ge(const_ready, 1)
            with pe.Fori(0, B) as b:
                pe.wait_ge(ln_z, 2 * b + 2 + Z_FREE)
                for c in range(CH):
                    pe.wait_ge(y4_done, CH * b + c - 1 + Y_FREE)
                    for tt in range(TT):
                        last = tr(ps_pt[c % 2][:, tt * P:(tt + 1) * P], z2[:, tt, c * P:(c + 1) * P], ident[:])
                    last.then_inc(zt_done, 1)

            def w_at(par, part, c, at, n):
                start = part * PART + c * GW + at
                return w_bf[:, bass.ds(par * PAR, PAR)][:, start:start + n]

            def project(b, i, half, par, t):
                c0 = i % TT
                tok = slice(b * T + c0 * P, b * T + (c0 + 1) * P)
                dst = tile_bank(i, t)
                if half == 0 and at_start(t):
                    if t >= len(START_BANKS):
                        pe.wait_ge(qn_done, t + 1 - len(START_BANKS))
                elif half == 0:
                    pe.wait_ge(qn_done, t - 1)
                cross = i >= TT
                jobs = []
                if not cross:
                    jobs.append((0, 256, [(xq[:, 0, c, tok], c, part) for c in range(CH) for part in range(2)]))
                    jobs.append((256, 128, [(xq[:, 2, c, tok], c, part) for c in range(CH) for part in range(2)]))
                    jobs.append((384, 128, [(xq[:, 3, c, tok], c, part) for c in range(CH) for part in range(2)]))
                else:
                    jobs.append((0, 256, [(xq[:, 1, c, tok], c, part) for c in range(CH) for part in range(2)]))
                    jobs.append((256, 256, [(ctx_hi[:, c, tok], c, part) for c in range(CH) for part in range(2)] +
                                           [(ctx_lo[:, c, tok], c, 0) for c in range(CH)]))
                for at, n, terms in (jobs[:1] if half == 0 else jobs[1:]):
                    for k, (lhs, c, part) in enumerate(terms):
                        last = mm(dst[:, at:at + n], lhs, w_at(par, part, c, cross * 512 + at, n),
                                  start=(k == 0), stop=(k == len(terms) - 1))
                if half == 1:
                    last.then_inc(proj_done, 1)

            def out_matmul(bank, tt, f):
                last = mm(bank[:], heads_in[:, f // HEADS, f % HEADS, tt * P:(tt + 1) * P], wp[:, f],
                          start=(f == 0), stop=(f == G * HEADS - 1))
                if f == G * HEADS - 1:
                    last.then_inc(pj_done, 1)

            def turn_qk(i, t):
                pe.wait_ge(qn_done, t + 1)
                pe.wait_ge(full_done, t)
                for h in range(3):
                    last = tr(ps_qt[:, h * D:(h + 1) * D], qn[:, i % 2, h * D:(h + 1) * D], ident[:])
                last.then_inc(qt_done, 1)

            pe.wait_ge(w_ready, CH + W_FREE)
            pe.wait_ge(xq_even, CH // 2)
            pe.wait_ge(xq_odd, CH // 2 + FREE)
            for i in range(TILES):
                if i == TT:
                    pe.wait_ge(ctx_lo_done, CH + FREE)
                for half in range(2):
                    project(0, i, half, 0, i)
                if i >= START_LAG:
                    turn_qk(i - START_LAG, i - START_LAG)
            for i in range(TILES - START_LAG, TILES):
                turn_qk(i, i)

            pe.wait_ge(xq_even, B * CH // 2)
            pe.wait_ge(xq_odd, B * CH // 2 + FREE)

            def group(g, first, last):
                for slot in slots(last):
                    for u in unit_at(slot, PV_LAG + TT - 1, first):
                        H, tc = u // TT, u % TT
                        b, head = H // HEADS, H % HEADS
                        cross = head // HPG
                        if tc == 0:
                            pe.wait_ge(ptlo_done, SLOTS * g + TT * (H + 1))
                            pe.wait_ge(y_done, GROUP_HEADS * g + H + FREE)
                        vh, vl = v_hi[:, b % 2, cross, tc], v_lo[:, b % 2, cross, tc]
                        ph, pl = pt_hi[:, H % 2, tc], pt_lo[:, H % 2, tc]
                        mm(ps_o[:], vh, ph, start=(tc == 0), stop=False)
                        mm(ps_o[:], vh, pl, start=False, stop=False)
                        last_mm = mm(ps_o[:], vl, ph, start=False, stop=(tc == TT - 1))
                        if tc == TT - 1:
                            last_mm.then_inc(pv_done, 1)
                    for k in tile_at(slot, QT_LAG, first, last):
                        turn_qk(tile_place(k)[1], GROUP_TILES * g + TILES + k)
                    k, half = slot // 2, slot % 2
                    if k < (GROUP_TILES - TILES if last else GROUP_TILES):
                        b, i = k // TILES, k % TILES
                        if k == GROUP_TILES - TILES and half == 0:
                            pe.wait_ge(w_ready, CH * g + 2 * CH + W_FREE)
                        project((b + 1) % B, i, half, (g + 1) % 2 if b == B - 1 else g % 2, GROUP_TILES * g + TILES + k)
                    if last and slot >= EARLY_FIRST:
                        if slot == EARLY_FIRST:
                            pe.wait_ge(early_done, EARLY_PIECES)
                            pe.wait_ge(stage_done, PROJ_PIECES)
                            pe.wait_ge(heads_back, 16)
                            pe.wait_ge(full_done, GROUP_TILES * G)
                            pe.wait_ge(qn_done, GROUP_TILES * G)
                        at = EARLY_STEP * (slot - EARLY_FIRST)
                        for n in range(at, min(at + EARLY_STEP, EARLY_TILES * G * HEADS)):
                            out_matmul(EARLY_BANKS[n // (G * HEADS)], n // (G * HEADS), n % (G * HEADS))
                    for u in unit_at(slot, 0, first):
                        b, head, qt = u // UNITS, u // TT % HEADS, u % TT
                        cross, hh = head // HPG, head % HPG
                        if u % (UNITS // 2) == 0:
                            pe.wait_ge(qklo_done, TILES * (B * g + b) + TT * (1 + cross))
                        if not first or u >= 2:
                            pe.wait_ge(exp_done, SLOTS * g + u - 1)
                        qs = slice(qt * P, (qt + 1) * P)
                        q_h, q_l = qk_hi[:, b % 2, cross, hh, qs], qk_lo[:, b % 2, cross, hh, qs]
                        k_h, k_l = qk_hi[:, b % 2, cross, 2], qk_lo[:, b % 2, cross, 2]
                        mm(ps_s[u % 2][:], q_h, k_h, start=True, stop=False)
                        mm(ps_s[u % 2][:], q_h, k_l, start=False, stop=False)
                        mm(ps_s[u % 2][:], q_l, k_h, start=False, stop=True).then_inc(s_done, 1)
                    for u in unit_at(slot, TURN_LAG, first):
                        pe.wait_ge(norm_done, SLOTS * g + u + 1)
                        if not first or u >= 2:
                            pe.wait_ge(ptlo_done, SLOTS * g + u - 1)
                        for tc in range(TT):
                            last_tr = tr(ps_pt[u % 2][:, tc * P:(tc + 1) * P], p_norm[:, u % 2, tc * P:(tc + 1) * P],
                                         ident[:])
                        last_tr.then_inc(pt_done, 1)

            group(0, True, False)
            with pe.Fori(1, G - 1) as g:
                group(g, False, False)
            group(G - 1, False, True)

            def out_projection(b):
                pe.wait_ge(heads_back, 16 * (b + 1))
                for tt in range(TT):
                    if tt >= 2:
                        pe.wait_ge(x1_done, TT * b + tt - 1)
                    for f in range(G * HEADS):
                        out_matmul(ps_s[tt % 2], tt, f)

            def turn_z(b):
                pe.wait_ge(ln_z, 2 * B + b + 1 + Z_FREE)
                for tt in range(TT):
                    if tt >= 2:
                        pe.wait_ge(ztlo_done, TT * b + tt - 1)
                    for c in range(CH):
                        last = tr(ps_pt[tt % 2][:, c * P:(c + 1) * P], z3[:, tt, c * P:(c + 1) * P], ident[:])
                    last.then_inc(z3t_done, 1)

            def gate_up(b):
                pe.wait_ge(ztlo_done, TT * (b + 1))
                for m in range(HC):
                    for k, bank, signal in ((0, ps_pj[m % 2], gate_done), (1, ps_up[m % 2], up_done)):
                        if m >= 2:
                            pe.wait_ge(hid_done, HC * b + m - 1)
                        for c in range(CH):
                            w = wgu[:, c, k * HID + m * P:k * HID + (m + 1) * P]
                            mm(bank[:], w, zt_hi[:, c], start=(c == 0), stop=False)
                            last = mm(bank[:], w, zt_lo[:, c], start=False, stop=(c == CH - 1))
                        last.then_inc(signal, 1)

            def down(b, overlapped):
                pe.wait_ge(hlo_done, HC * (b + 1))
                for tt in range(TT):
                    if tt >= 2:
                        pe.wait_ge(scaled_done, TT * b + tt - 1)
                    elif overlapped:
                        pe.wait_ge(x1_done, TT * (b + 1) + tt + 3)
                    for m in range(HC):
                        ts = slice(tt * P, (tt + 1) * P)
                        mm(ps_s[tt % 2][:], h_hi[:, m, ts], wd[:, m], start=(m == 0), stop=False)
                        last = mm(ps_s[tt % 2][:], h_lo[:, m, ts], wd[:, m], start=False, stop=(m == HC - 1))
                    last.then_inc(down_done, 1)

            for tt in range(EARLY_TILES, TT):
                for f in range(G * HEADS):
                    out_matmul(ps_s[tt % 2], tt, f)
            turn_z(0)
            pe.wait_ge(stage_done, N_STAGE)
            gate_up(0)
            with pe.Fori(1, B) as b:
                out_projection(b)
                down(b - 1, True)
                turn_z(b)
                gate_up(b)
            down(B - 1, False)

        @block.scalar
        def _(act):
            a = nc.scalar.activation
            act.sem_inc(y_done, FREE)
            act.sem_inc(y4_done, Y_FREE)

            def weight_hi(par, c, count):
                act.wait_ge(w_scaled, count)
                act.sem_inc(waited_act, 1)
                a(w_bf[:, bass.ds(par * PAR + c * GW, GW)], raw(c), ACT.Copy).then_inc(w_hi_done, 1)

            act.wait_ge(scales_ready, 1)

            def scale_chunk(b, c):
                act.wait_ge(zt_done, CH * b + c + 1)
                act.wait_ge(quant_step, QUANT_STEPS * (CH * b + c - 1) + QUANT_FREE)
                act.sem_inc(waited_act, 1)
                for s in range(SETS):
                    k = s * CH + c
                    last = a(y4[:, c % 2, s * T:(s + 1) * T], ps_pt[c % 2][:], ACT.Identity,
                             scale=ln_scale[:, k:k + 1], bias=ln_bias[:, k:k + 1])
                last.then_inc(y4_done, 1)

            def ctx_part(b):
                act.wait_ge(ctx_loaded, 16 * (b + 1))
                act.sem_inc(waited_act, 1)
                a(ctx_hi[:, bass.ds(b, 1)].rearrange("p o t -> p (o t)"), ctx_raw[:], ACT.Copy).then_inc(ctx_hi_done, 1)

            with act.Fori(0, B - 1) as b:
                scale_chunk(b, 0)
                weight_hi(0, b, b + 1)
                scale_chunk(b, 1)
                ctx_part(b)
                scale_chunk(b, 2)
                scale_chunk(b, 3)

            def squares(i, t):
                act.wait_ge(proj_done, t + 1)
                act.wait_ge(red_done, t)
                a(sq[:], tile_bank(i, t)[:, 0:3 * D], ACT.Square).then_inc(sq_done, 1)

            def v_part(b, i, t):
                a(v_hi[:, b % 2, i // TT, i % TT], tile_bank(i, t)[:, 3 * D:4 * D], ACT.Copy).then_inc(vhi_done, 1)

            def qk_part(b, i, t):
                act.wait_ge(qt_done, t + 1)
                if not at_start(t):
                    act.wait_ge(qklo_done, t)
                elif t >= 2:
                    act.wait_ge(qklo_done, t - 1)
                full = full_of(i, t)
                cross, ts = i // TT, slice((i % TT) * P, (i % TT + 1) * P)
                w, bias = qscaled[:, 2 * cross:2 * cross + 1], qscaled[:, 2 * cross + 1:2 * cross + 2]
                kw, kb = ("kxln_w", "kxln_b") if cross else ("kln_w", "kln_b")
                q_in, k_in = ps_qt[:, 0:2 * D], ps_qt[:, 2 * D:3 * D]
                a(qk_hi[:, b % 2, cross, 0:2, ts], q_in.rearrange("p (h t) -> p h t", h=2), ACT.Identity, bias=bias, scale=w)
                a(qk_hi[:, b % 2, cross, 2, ts], k_in, ACT.Identity, bias=c_(kb), scale=c_(kw))
                a(full[:, 0:2 * D], q_in, ACT.Identity, bias=bias, scale=w)
                a(full[:, 2 * D:3 * D], k_in, ACT.Identity, bias=c_(kb), scale=c_(kw)).then_inc(full_done, 1)

            scale_chunk(B - 1, 0)
            weight_hi(0, B - 1, B)
            scale_chunk(B - 1, 1)
            ctx_part(B - 1)
            scale_chunk(B - 1, 2)
            act.wait_ge(zt_done, B * CH)
            squares(0, 0)
            v_part(0, 0, 0)
            scale_chunk(B - 1, 3)
            for i in range(TILES):
                if i >= 1:
                    squares(i, i)
                    v_part(0, i, i)
                if i >= START_LAG:
                    qk_part(0, i - START_LAG, i - START_LAG)
            for i in range(TILES - START_LAG, TILES):
                qk_part(0, i, i)
            act.wait_ge(xq_odd, B * CH // 2 + FREE)
            act.wait_ge(xq_even, B * CH // 2)

            def convert(n):
                src, dst, offset = stage_pieces(w_proj, w_gate, w_up, w_down)[n]
                act.wait_ge(stage_loaded[n % 2], 16 * (n // 2 + 1))
                rows, width = src.shape[1], src.shape[2]
                raw = stage[:, n % 2, 0:rows * width].bitcast(src.dtype).rearrange("p (r w) -> p r w", w=width)
                a(dst, raw, ACT.Copy, bias=offset).then_inc(stage_done, 1)

            def group(g, first, last):
                for slot in slots(last):
                    for k in tile_at(slot, SQ_LAG, first, last):
                        b, i = tile_place(k)
                        t = GROUP_TILES * g + TILES + k
                        squares(i, t)
                        v_part(b, i, t)
                    for u in unit_at(slot, HI_LAG, first):
                        H, qt = u // TT, u % TT
                        act.wait_ge(pt_done, SLOTS * g + u + 1)
                        if qt == 0 and (not first or H >= 2):
                            act.wait_ge(pv_done, GROUP_HEADS * g + H - 1)
                        a(pt_hi[:, H % 2, :, qt * P:(qt + 1) * P], ps_pt[u % 2].rearrange("p (c t) -> p c t", c=TT),
                          ACT.Copy).then_inc(pthi_done, 1)
                    for k in tile_at(slot, QK_LAG, first, last):
                        qk_part(*tile_place(k), GROUP_TILES * g + TILES + k)
                    for H in head_at(slot, Y_LAG, first):
                        act.wait_ge(pv_done, GROUP_HEADS * g + H + 1)
                        if not first or H >= 2:
                            act.wait_ge(heads_done, GROUP_HEADS * g + H - 1)
                        act.sem_inc(waited_act, 1)
                        column = HEADS * (g + H // GROUP_HEADS) + H % HEADS
                        a(y[:, H % 2], ps_o[:], ACT.Copy, scale=rsmooth[:, bass.ds(column, 1)]).then_inc(y_done, 1)
                    for c in prep_at(slot, W_HI_LAG, last):
                        weight_hi((g + 1) % 2, c, CH * g + CH + c + 1)
                    for u in unit_at(slot, EXP_LAG, first):
                        act.wait_ge(max_done, SLOTS * g + u + 1)
                        if not first or u >= 2:
                            act.wait_ge(norm_done, SLOTS * g + u - 1)
                        a(p_exp[:, u % 2], ps_s[u % 2][:], ACT.Exp, bias=neg_max[:, u % 4:u % 4 + 1],
                          accum_out=p_sum[:, u % 4:u % 4 + 1]).then_inc(exp_done, 1)
                    if last and slot - CONVERT_LAG in EARLY_SLOTS:
                        n = EARLY_SLOTS.index(slot - CONVERT_LAG)
                        act.wait_ge(w_loaded, 16 * (CH * G + n + 1 + FREE))
                        src, dst = early_piece(n)
                        a(dst, raw(n).rearrange("p (r w) -> p r w", w=DM), ACT.Copy).then_inc(early_done, 1)
                    if last and slot in CONVERT_SLOTS:
                        convert(CONVERT_SLOTS.index(slot))

            group(0, True, False)
            with act.Fori(1, G - 1) as g:
                group(g, False, False)
            group(G - 1, False, True)
            for n in range(len(CONVERT_SLOTS), N_STAGE):
                convert(n)

            def finish(b):
                for tt in range(TT):
                    act.wait_ge(z3t_done, TT * b + tt + 1)
                    a(zt_hi[:, :, tt * P:(tt + 1) * P], ps_pt[tt % 2].rearrange("p (c t) -> p c t", c=CH), ACT.Copy)\
                        .then_inc(zthi_done, 1)

                def h_part(m):
                    act.wait_ge(hid_done, HC * b + m + 1)
                    a(h_hi[:, m], hid[:, m % 2], ACT.Copy).then_inc(hhi_done, 1)

                for m in range(HC):
                    act.wait_ge(gate_done, HC * b + m + 1)
                    if m >= 2:
                        act.wait_ge(hid_done, HC * b + m - 1)
                    a(silu[:, m % 2], ps_pj[m % 2][:], ACT.Silu, scale=c_("s_gate", m)).then_inc(silu_done, 1)
                    if m >= 1:
                        h_part(m - 1)
                h_part(HC - 1)

            with act.Fori(0, B) as b:
                finish(b)

        @block.gpsimd
        def _(pool):
            nc.gpsimd.memset(ident[:], 0.0).then_inc(ident_zero, 1)
            pool.wait_ge(ident_zero, 1)
            nc.gpsimd.affine_select(out=ident[:], in_=ident[:], compare_op=ALU.not_equal, fill=1.0, base=0,
                                    pattern=[[-1, P]], channel_multiplier=1).then_inc(const_ready, 1)
            nc.gpsimd.memset(minus_half[:], -0.5).then_inc(const_ready, 1)
            tt_ = nc.gpsimd.tensor_tensor

            def spread_cols(v):
                return v.unsqueeze(2).to_broadcast([P, 8, D])

            def by_head(c):
                return raw(c).rearrange("p (k d) -> p k d", k=8)

            def weight_centre(c, count):
                pool.wait_ge(w_step, 2 * count)
                tt_(by_head(c), by_head(c), spread_cols(w_mean[:]), ALU.subtract).then_inc(w_centred, 1)

            def weight_scale(c, count):
                pool.wait_ge(w_centred, count)
                tt_(by_head(c), by_head(c), spread_cols(wscale[:, bass.ds(8 * c, 8)]), ALU.mult).then_inc(w_scaled, 1)

            def power(n):
                pool.wait_ge(ln_var, n + 1)
                tt_(rstd[:], spread[:], minus_half[:, 0:TT], ALU.pow).then_inc(ln_rstd, 1)

            pool.wait_ge(const_ready, 2)
            pool.wait_ge(scales_ready, 1)
            def odd_chunk(b, c):
                pool.wait_ge(quant_step, QUANT_STEPS * (CH * b + c + 1) + QUANT_FREE)
                tt_(xq[:, :, c, bass.ds(b * T, T)], sum4[:, 1].rearrange("p (s t) -> p s t", t=T),
                    mag4[:, 1].rearrange("p (s t) -> p s t", t=T), ALU.subtract).then_inc(xq_odd, 1)

            pool.sem_inc(xq_odd, FREE)
            def prepare_weights(b):
                weight_centre(b, b + 1)
                weight_scale(b, b + 1)

            def rests(b):
                pool.wait_ge(w_hi_done, b + 1)
                tt_(w_bf[:, bass.ds(b * GW + PART, GW)], raw(b), w_bf[:, bass.ds(b * GW, GW)], ALU.subtract)\
                    .then_inc(w_ready, 1)
                pool.wait_ge(ctx_hi_done, b + 1)
                tt_(ctx_lo[:, bass.ds(b, 1)].rearrange("p o t -> p (o t)"), ctx_raw[:],
                    ctx_hi[:, bass.ds(b, 1)].rearrange("p o t -> p (o t)"), ALU.subtract).then_inc(ctx_lo_done, 1)

            power(0)
            power(1)
            prepare_weights(0)
            with pool.Fori(0, B - 1) as b:
                power(2 * b + 2)
                rests(b)
                odd_chunk(b, 1)
                power(2 * b + 3)
                prepare_weights(b + 1)
                odd_chunk(b, 3)
            rests(B - 1)

            def head_power(i, t):
                pool.wait_ge(var_done, t + 1)
                tt_(head_rstd[:, i % 2, 0:3], head_var[:, i % 2, 0:3], minus_half[:, 0:3], ALU.pow).then_inc(rstd_done, 1)

            def qk_rest(b, i, t):
                pool.wait_ge(full_done, t + 1)
                cross, ts = i // TT, slice((i % TT) * P, (i % TT + 1) * P)
                tt_(qk_lo[:, b % 2, cross, :, ts], full_of(i, t).rearrange("p (h t) -> p h t", h=3),
                    qk_hi[:, b % 2, cross, :, ts], ALU.subtract).then_inc(qklo_done, 1)

            for i in range(TILES):
                head_power(i, i)
                if i >= START_LAG:
                    qk_rest(0, i - START_LAG, i - START_LAG)
            for i in range(TILES - START_LAG, TILES):
                qk_rest(0, i, i)
            pool.wait_ge(qklo_done, TILES)

            def group(g, first, last):
                for slot in slots(last):
                    for c in prep_at(slot, CENTRE_LAG, last):
                        weight_centre(c, CH * g + CH + c + 1)
                    for c in prep_at(slot, SCALE_LAG, last):
                        weight_scale(c, CH * g + CH + c + 1)
                    for k in tile_at(slot, VAR_LAG, first, last):
                        head_power(tile_place(k)[1], GROUP_TILES * g + TILES + k)
                    for u in unit_at(slot, NORM_LAG, first):
                        pool.wait_ge(rsum_done, SLOTS * g + u + 1)
                        if not first or u >= 2:
                            pool.wait_ge(pt_done, SLOTS * g + u - 1)
                        tt_(p_norm[:, u % 2], p_exp[:, u % 2], r_sum[:, u % 4:u % 4 + 1].to_broadcast([P, T]), ALU.mult)\
                            .then_inc(norm_done, 1)
                    for k in tile_at(slot, REST_LAG, first, last):
                        qk_rest(*tile_place(k), GROUP_TILES * g + TILES + k)

            group(0, True, False)
            with pool.Fori(1, G - 1) as g:
                group(g, False, False)
            group(G - 1, False, True)

            with pool.Fori(0, B) as b:
                power(2 * B + b)
                for m in range(HC):
                    pool.wait_ge(hhi_done, HC * b + m + 1)
                    tt_(h_lo[:, m], hid[:, m % 2], h_hi[:, m], ALU.subtract).then_inc(hlo_done, 1)

        @block.vector
        def _(dve):
            v = nc.vector
            dve.sem_inc(w_ready, W_FREE)
            dve.sem_inc(ln_z, Z_FREE)
            dve.sem_inc(quant_step, QUANT_FREE)
            dve.sem_inc(ctx_lo_done, FREE)
            v.memset(centre[:], 1.0 / D).then_inc(ones_set, 1)
            dve.wait_ge(ones_set, 1)
            dve.wait_ge(cols_in, 16)
            v.reciprocal(rscale, c_("in_scale", 0, SETS * CH)).then_inc(ones_set, 1)
            v.reciprocal(rsmooth[:], c_("smooth", 0, NH * 2))
            v.tensor_tensor(pscale[:], c_("proj_in"), c_("proj_w"), ALU.mult)
            for k, name in enumerate(("qln_w", "qln_b", "qxln_w", "qxln_b")):
                v.tensor_scalar(qscaled[:, k:k + 1], c_(name), float(D) ** -0.5, None, ALU.mult)
            v.memset(centre[:, 3:4], 0.0)
            v.memset(centre[:, 7:8], 0.0)
            v.memset(wscale[:], 1.0).then_inc(ones_set, 1)
            dve.wait_ge(ones_set, 3)
            for s in range(SETS):
                sets = slice(s * CH, (s + 1) * CH)
                v.tensor_tensor(ln_scale[:, sets], c_("ln_w", 0, CH), rscale[:, sets], ALU.mult)
                v.tensor_tensor(ln_bias[:, sets], c_("ln_b", 0, CH), rscale[:, sets], ALU.mult)
            for k, s in ((0, 0), (1, 0), (2, 2), (3, 3), (4, 1), (5, 1)):
                last = v.tensor_scalar(wscale[:].rearrange("p (c k) -> p c k", k=8)[:, :, k], c_("in_scale", s * CH, CH),
                                       c_("w_scale", s), None, ALU.mult)
            last.then_inc(scales_ready, 1)
            dve.wait_ge(scales_ready, 1)

            def weight_sums(c, count):
                dve.wait_ge(w_loaded, 16 * (count + FREE))
                v.tensor_reduce(w_sum[:], raw(c).rearrange("p (k d) -> p k d", k=8), AX_X, ALU.add).then_inc(w_step, 1)
                dve.wait_ge(w_step, 2 * count - 1)
                v.tensor_tensor(w_mean[:], w_sum[:], centre[:], ALU.mult).then_inc(w_step, 1)

            def weight_lo(par, c, count):
                dve.wait_ge(w_hi_done, count)
                hi = w_bf[:, bass.ds(par * PAR + c * GW, GW)]
                lo = w_bf[:, bass.ds(par * PAR + c * GW + PART, GW)]
                v.tensor_tensor(lo, raw(c), hi, ALU.subtract).then_inc(w_ready, 1)

            def ln_stats(src):
                for tt in range(TT):
                    v.bn_stats(stats[:, tt], src(tt)).then_inc(ln_step, 1)

            def ln_variance(n):
                dve.wait_ge(ln_step, LN_STEPS * n + TT)
                dve.sem_inc(waited_dve, 1)
                for tt in range(TT):
                    v.bn_aggr(moments[:, tt], stats[:, tt]).then_inc(ln_step, 1)
                dve.wait_ge(ln_step, LN_STEPS * (n + 1))
                v.tensor_scalar(spread[:], moments[:, :, 1], EPS, None, ALU.add).then_inc(ln_var, 1)

            def ln_apply(n, src, dst):
                dve.wait_ge(ln_rstd, n + 1)
                for tt in range(TT):
                    last = v.tensor_scalar(dst[:, tt], src(tt), moments[:, tt, 0:1], rstd[:, tt:tt + 1],
                                           ALU.subtract, ALU.mult)
                last.then_inc(ln_z, 1)

            def layer_norm(n, src, dst):
                ln_stats(src)
                ln_variance(n)
                ln_apply(n, src, dst)

            def quantise(n, val, magnitude, total, free=None):
                at = QUANT_STEPS * n + QUANT_FREE
                v.tensor_scalar(val, val, FP8_MAX, -FP8_MAX, ALU.min, ALU.max).then_inc(quant_step, 1)
                dve.wait_ge(quant_step, at + 1)
                if free:
                    free()
                v.tensor_scalar(magnitude.bitcast(I16), val.bitcast(I16), EXPONENT, None, ALU.bitwise_and)\
                    .then_inc(quant_step, 1)
                dve.wait_ge(quant_step, at + 2)
                v.tensor_scalar(magnitude, magnitude, MIN_BINADE, KEEP4, ALU.max, ALU.mult).then_inc(quant_step, 1)
                dve.wait_ge(quant_step, at + 3)
                v.tensor_tensor(total, val, magnitude, ALU.add).then_inc(quant_step, 1)

            def x_at(b):
                xb = local[:, bass.ds((b % 2) * (2 * TT * DM), 2 * TT * DM)].bitcast(F32)
                return lambda tt: xb[:, tt * DM:(tt + 1) * DM]

            def z1_at(tt):
                return z1[:, tt]

            def quantise_chunk(b, c, own=False):
                n = CH * b + c
                dve.wait_ge(y4_done, n + 1 + Y_FREE)

                def free():
                    if c % 2:
                        dve.wait_ge(xq_odd, CH // 2 * b + c // 2 + FREE)
                quantise(n, y4[:, c % 2], mag4[:, c % 2], sum4[:, c % 2], free)
                if own or c % 2 == 0:
                    dve.wait_ge(quant_step, QUANT_STEPS * (n + 1) + QUANT_FREE)
                    v.tensor_tensor(xq[:, :, c, bass.ds(b * T, T)], sum4[:, c % 2].rearrange("p (s t) -> p s t", t=T),
                                    mag4[:, c % 2].rearrange("p (s t) -> p s t", t=T), ALU.subtract)\
                        .then_inc(xq_odd if c % 2 else xq_even, 1)

            dve.wait_ge(x_loaded, 16 * (1 + FREE))
            layer_norm(0, x_at(0), z1)
            dve.wait_ge(ln_z, 1 + Z_FREE)
            layer_norm(1, z1_at, z2)
            weight_sums(0, 1)
            with dve.Fori(0, B - 1) as b:
                n = 2 * b + 2
                dve.wait_ge(x_loaded, 16 * (b + 2 + FREE))
                dve.sem_inc(waited_dve, 1)
                ln_stats(x_at(b + 1))
                quantise_chunk(b, 0)
                ln_variance(n)
                quantise_chunk(b, 1)
                ln_apply(n, x_at(b + 1), z1)
                dve.wait_ge(ln_z, n + 1 + Z_FREE)
                dve.sem_inc(waited_dve, 1)
                ln_stats(z1_at)
                quantise_chunk(b, 2)
                ln_variance(n + 1)
                dve.wait_ge(w_centred, b + 1)
                weight_sums(b + 1, b + 2)
                dve.wait_ge(zt_done, CH * (b + 1))
                ln_apply(n + 1, z1_at, z2)
                quantise_chunk(b, 3)

            def head_variance(i, t):
                dve.wait_ge(sq_done, t + 1)
                v.tensor_reduce(sq_sum[:, i % 2, 0:3], sq[:].rearrange("p (h d) -> p h d", h=3), AX_X, ALU.add)\
                    .then_inc(red_done, 1)
                dve.wait_ge(red_done, t + 1)
                v.tensor_scalar(head_var[:, i % 2, 0:3], sq_sum[:, i % 2, 0:3], 1.0 / D, EPS, ALU.mult, ALU.add)\
                    .then_inc(var_done, 1)

            def v_rest(b, i, t):
                dve.wait_ge(vhi_done, t + 1)
                v.tensor_tensor(v_lo[:, b % 2, i // TT, i % TT], tile_bank(i, t)[:, 3 * D:4 * D],
                                v_hi[:, b % 2, i // TT, i % TT], ALU.subtract).then_inc(vlo_done, 1)

            def head_norm(i, t):
                dve.wait_ge(rstd_done, t + 1)
                if not isinstance(t, int) or t >= 2:
                    dve.wait_ge(qt_done, t - 1)
                v.tensor_tensor(qn[:, i % 2].rearrange("p (h d) -> p h d", h=3),
                                tile_bank(i, t)[:, 0:3 * D].rearrange("p (h d) -> p h d", h=3),
                                head_rstd[:, i % 2, 0:3].unsqueeze(2).to_broadcast([P, 3, D]), ALU.mult)\
                    .then_inc(qn_done, 1)

            quantise_chunk(B - 1, 0, True)
            quantise_chunk(B - 1, 1, True)
            for i in range(TILES):
                head_variance(i, i)
                v_rest(0, i, i)
                if i >= 1:
                    head_norm(i - 1, i - 1)
                if i < 2:
                    quantise_chunk(B - 1, 2 + i, True)
            head_norm(TILES - 1, TILES - 1)

            def group(g, first, last):
                for slot in slots(last):
                    for c in prep_at(slot, SUMS_LAG, last):
                        weight_sums(c, CH * g + CH + c + 1)
                    for u in unit_at(slot, MAX_LAG, first):
                        dve.wait_ge(s_done, SLOTS * g + u + 1)
                        v.tensor_reduce(neg_max[:, u % 4:u % 4 + 1], ps_s[u % 2][:], AX_X, ALU.max, negate=True)\
                            .then_inc(max_done, 1)
                    for H in head_at(slot, QUANT_LAG, first):
                        head = H % HEADS
                        dve.wait_ge(y_done, GROUP_HEADS * g + H + 1 + FREE)

                        def stored():
                            if head == 0:
                                dve.wait_ge(heads_stored, 16 * (B * g + H // HEADS + FREE))
                        n = B * CH + GROUP_HEADS * g + H
                        quantise(n, y[:, H % 2], mag, summed)
                        dve.wait_ge(quant_step, QUANT_STEPS * (n + 1) + QUANT_FREE)
                        stored()
                        v.tensor_tensor(heads[:, head], summed, mag, ALU.subtract).then_inc(heads_done, 1)
                    for u in unit_at(slot, SUM_LAG, first):
                        dve.wait_ge(exp_done, SLOTS * g + u + 1)
                        v.reciprocal(r_sum[:, u % 4:u % 4 + 1], p_sum[:, u % 4:u % 4 + 1]).then_inc(rsum_done, 1)
                    for c in prep_at(slot, W_LO_LAG, last):
                        weight_lo((g + 1) % 2, c, CH * g + CH + c + 1)
                    for k in tile_at(slot, QN_LAG, first, last):
                        head_norm(tile_place(k)[1], GROUP_TILES * g + TILES + k)
                    for k in tile_at(slot, VAR_LAG, first, last):
                        head_variance(tile_place(k)[1], GROUP_TILES * g + TILES + k)
                    for u in unit_at(slot, LO_LAG, first):
                        H, qt = u // TT, u % TT
                        dve.wait_ge(pthi_done, SLOTS * g + u + 1)
                        dst = slice(qt * P, (qt + 1) * P)
                        v.tensor_tensor(pt_lo[:, H % 2, :, dst], ps_pt[u % 2].rearrange("p (c t) -> p c t", c=TT),
                                        pt_hi[:, H % 2, :, dst], ALU.subtract).then_inc(ptlo_done, 1)
                    for k in tile_at(slot, VAR_LAG, first, last):
                        v_rest(*tile_place(k), GROUP_TILES * g + TILES + k)

            group(0, True, False)
            with dve.Fori(1, G - 1) as g:
                group(g, False, False)
            group(G - 1, False, True)

            def x1_at(b, tt):
                if isinstance(b, int):
                    at = (b % 2) * TT * DM + tt * DM
                    return x1[:, at:at + DM]
                return x1[:, bass.ds((b % 2) * (TT * DM) + tt * DM, DM)]

            def residual(b, banks):
                dve.wait_ge(x_back, 16 * (b + 1))
                for tt in range(TT):
                    dve.wait_ge(pj_done, TT * b + tt + 1)
                    v.scalar_tensor_tensor(x1_at(b, tt), banks[tt][:], pscale[:, 0:1], x_res[:, tt], ALU.mult, ALU.add)\
                        .then_inc(x1_done, 1)
                dve.wait_ge(x1_done, TT * (b + 1))
                dve.sem_inc(waited_dve, 1)
                layer_norm(2 * B + b, lambda tt: x1_at(b, tt), z3)

            def output(b):
                dve.wait_ge(sdown_in, 16)
                for tt in range(TT):
                    dve.wait_ge(down_done, TT * b + tt + 1)
                    v.tensor_tensor(scaled[:, tt % 2], ps_s[tt % 2][:], sdown[:], ALU.mult).then_inc(scaled_done, 1)
                    dve.wait_ge(scaled_done, TT * b + tt + 1)
                    dve.wait_ge(out_stored[tt % 2], 16 * (TT // 2 * b + tt // 2 + FREE))
                    v.tensor_tensor(y_out[:, tt % 2], scaled[:, tt % 2], x1_at(b, tt), ALU.add).then_inc(out_ready, 1)

            def hidden(b):
                for tt in range(TT):
                    dve.wait_ge(zthi_done, TT * b + tt + 1)
                    dst = slice(tt * P, (tt + 1) * P)
                    v.tensor_tensor(zt_lo[:, :, dst], ps_pt[tt % 2].rearrange("p (c t) -> p c t", c=CH), zt_hi[:, :, dst],
                                    ALU.subtract).then_inc(ztlo_done, 1)
                for m in range(HC):
                    dve.wait_ge(silu_done, HC * b + m + 1)
                    dve.wait_ge(up_done, HC * b + m + 1)
                    if m >= 2:
                        dve.wait_ge(hlo_done, HC * b + m - 1)
                    v.scalar_tensor_tensor(hid[:, m % 2], ps_up[m % 2][:], c_("s_up", m), silu[:, m % 2],
                                           ALU.mult, ALU.mult).then_inc(hid_done, 1)

            residual(0, [*EARLY_BANKS, ps_s[EARLY_TILES % 2]])
            hidden(0)
            with dve.Fori(1, B) as b:
                residual(b, ps_s * 2)
                output(b - 1)
                hidden(b)
            output(B - 1)


def kernel(**inputs):
    import concourse.bacc as bacc
    from concourse.bass_utils import run_bass_kernel_spmd

    a = {k: np.asarray(v) for k, v in inputs.items()}
    xa = {k[len("L0_xattn_"):]: v for k, v in a.items() if k.startswith("L0_xattn_")}
    ff = {k[len("L0_ffn_"):]: v for k, v in a.items() if k.startswith("L0_ffn_")}

    def per_group(w, n):
        return w.reshape(G, n, DM).transpose(0, 2, 1)

    kvx = xa["w_kv_x"]
    w_group = np.concatenate([per_group(xa["wq"], 256), per_group(xa["wk"], 128), per_group(xa["wv"], 128),
                              per_group(xa["wqx"], 256), per_group(kvx[:G * D], 128), per_group(kvx[G * D:], 128)], axis=2)
    order = [f for g in range(G) for f in (2 * g, 2 * g + 1, NH + 2 * g, NH + 2 * g + 1)]
    w_proj = xa["wproj"].T.reshape(2 * NH, D, DM)[order].reshape(2 * NH * D, DM)
    smooth = xa["proj_smooth"].reshape(2 * NH, D)[order]

    def column(v):
        return np.broadcast_to(v.reshape(1, 1), (P, 1))

    def chunked(v):
        return v.reshape(-1, P).T

    parts = {
        "ln_w": chunked(xa["ln_w"]), "ln_b": chunked(xa["ln_b"]),
        "in_scale": np.concatenate([chunked(xa[f"{n}_in_scale"]) for n in ("q", "qx", "k", "v")], axis=1),
        "w_scale": np.concatenate([column(xa[f"w{n}_scale"]) for n in ("q", "qx", "k", "v")], axis=1),
        **{n: chunked(xa[n]) for n in ("qln_w", "qln_b", "qxln_w", "qxln_b", "kln_w", "kln_b", "kxln_w", "kxln_b")},
        "smooth": smooth.T, "s_gate": chunked(ff["s_gate"]), "s_up": chunked(ff["s_up"]),
        "proj_in": column(xa["proj_in_scale"]), "proj_w": column(xa["proj_w_scale"]),
    }
    arrays = {
        "x": a["x"].reshape(NTOK, DM),
        "ctx_t": a["ctx_2048"].reshape(NTOK, DM).T,
        "w_group": w_group,
        "w_proj": w_proj,
        "w_gate": ff["wq_gate"].T,
        "w_up": ff["wq_up"].T,
        "w_down": ff["wq_down"].T,
        "cols": np.concatenate([parts[n] for n in COLS], axis=1),
        "s_down": np.broadcast_to(ff["s_down"].reshape(1, DM), (P, DM)),
    }
    arrays = {k: np.ascontiguousarray(v) for k, v in arrays.items()}

    nc = bacc.Bacc("TRN2", target_bir_lowering=False, num_devices=1)
    args = [nc.dram_tensor(n, v.shape, mybir.dt.from_np(v.dtype), kind="ExternalInput").ap() for n, v in arrays.items()]
    out = nc.dram_tensor("out", (NTOK, DM), F32, kind="ExternalOutput").ap()
    block_kernel(nc, *args, out)
    r = run_bass_kernel_spmd(nc, [arrays], core_ids=[0])
    return r.results[0]["out"].reshape(B, T, DM)
```
